# Optimizing a Trainium2 kernel written in Bass

```python
import numpy as np
import jax
import jax.numpy as jnp

def _softmax(x, axis=-1):
    return jax.nn.softmax(x, axis=axis)

def _gelu(x):
    return jax.nn.gelu(x, approximate=True)

def _silu(x):
    return jax.nn.silu(x)

def _sigmoid(x):
    return jax.nn.sigmoid(x)

def _layernorm(x, axis=-1, eps=1e-05):
    m = jnp.mean(x, axis=axis, keepdims=True)
    v = jnp.var(x, axis=axis, keepdims=True)
    return (x - m) / jnp.sqrt(v + eps)

def _scatter_add(tgt, idx, src, axis=0):
    return tgt.at[idx].add(src)

def _segment_sum(src, seg, n):
    return jax.ops.segment_sum(src, seg, n)
kernel_name = 'mk_xattn_ffn_d1_seqx_r4_d2e53b'

def setup_inputs(seed: int=0):
    np.random.seed(seed)
    _w = jnp.asarray

    def _rec_inputs():
        import jax
        import jax.numpy as jnp
        _rk = jax.random.key(seed)
        x = 7.22e-05 + 1 * jax.random.normal(jax.random.fold_in(_rk, 1), (4, 1024, 256), jnp.float32)
        _lenS = 1024 - jax.random.randint(jax.random.fold_in(_rk, 7), (4,), 0, max(1, 1024 // 4) + 1, jnp.int32)
        _lenS2 = 154 - jax.random.randint(jax.random.fold_in(_rk, 8), (4,), 0, max(1, 154 // 4) + 1, jnp.int32)
        _ctx_1024P = jax.random.normal(jax.random.fold_in(_rk, 11), (4, 16, 256), jnp.float32)
        _ctx_1024c = jax.random.dirichlet(jax.random.fold_in(_rk, 511), 0.3 * jnp.ones((16,), jnp.float32), (4, 154))
        _ctx_1024t = jnp.einsum('bsk,bkd->bsd', _ctx_1024c, _ctx_1024P)
        _ctx_1024t = _ctx_1024t * jax.lax.rsqrt(jnp.mean(jnp.square(_ctx_1024t)) + 1e-12) * 0.953939
        ctx_1024 = 4.13588e-05 + 0.999923 * (_ctx_1024t + 0.3 * jax.random.normal(jax.random.fold_in(_rk, 611), (4, 154, 256), jnp.float32))
        _validS = jnp.arange(1024)[None, :] < _lenS[:, None]
        _validS2 = jnp.arange(154)[None, :] < _lenS2[:, None]
        _causal = jnp.tril(jnp.ones((1024, 1024), dtype=bool))
        mask_1x1xSxS2_bk0 = jnp.logical_not(jnp.broadcast_to(_validS2[0:1, None, None, :], (1, 1, 1024, 154)))
        return (x, ctx_1024, mask_1x1xSxS2_bk0)
    x, ctx_1024, mask_1x1xSxS2_bk0 = _rec_inputs()

    def _L0_xattn_setup():
        import jax, jax.numpy as jnp
        import numpy as np
        D_MODEL = 256
        NUM_HEADS = 16
        HEAD_DIM = D_MODEL // NUM_HEADS
        key = jax.random.key(seed)
        kq, kk, kv, k1, k2, k3, k4 = jax.random.split(key, 7)
        B, S = (4, 512)
        scale = 1.0 / np.sqrt(D_MODEL)
        return {'q': jax.random.normal(kq, (B, S, D_MODEL), jnp.float32), 'k': jax.random.normal(kk, (B, S, D_MODEL), jnp.float32), 'v': jax.random.normal(kv, (B, S, D_MODEL), jnp.float32), 'mask': jnp.tril(jnp.ones((S, S), jnp.bool_))[None, None, :, :], 'W_q': jax.random.normal(k1, (D_MODEL, D_MODEL), jnp.float32) * scale, 'W_k': jax.random.normal(k2, (D_MODEL, D_MODEL), jnp.float32) * scale, 'W_v': jax.random.normal(k3, (D_MODEL, D_MODEL), jnp.float32) * scale, 'W_o': jax.random.normal(k4, (D_MODEL, D_MODEL), jnp.float32) * scale}
    _L0_xattn_all = _L0_xattn_setup()
    _L0_xattn_in = {k: v for k, v in _L0_xattn_all.items() if k in ('W_q', 'W_k', 'W_v', 'W_o')}
    del _L0_xattn_all

    def _L0_ffn_setup():
        import jax, jax.numpy as jnp
        import numpy as np
        B, L, H = (32, 128, 256)
        E, R, TOP_K = (8, 16, 2)

        def _gates(cls, router_w):
            logits = jnp.einsum('bh,eh->be', cls, router_w)
            top_vals, top_idx = jax.lax.top_k(logits, TOP_K)
            mask = jnp.full_like(logits, -jnp.inf)
            rows = jnp.arange(logits.shape[0])[:, None]
            mask = mask.at[rows, top_idx].set(top_vals)
            return jax.nn.softmax(mask, axis=1)
        key = jax.random.key(seed)
        k1, k2, k3, k4 = jax.random.split(key, 4)
        x = jax.random.normal(k1, (B, L, H), dtype=jnp.float32)
        router_w = jax.random.normal(k2, (E, H), dtype=jnp.float32) * 0.02
        lora_down = jax.random.normal(k3, (E, R, H), dtype=jnp.float32) * (1.0 / np.sqrt(H))
        lora_up = jax.random.normal(k4, (E, H, R), dtype=jnp.float32) * (1.0 / np.sqrt(R))
        return {'x': x, 'router_w': router_w, 'lora_down': lora_down, 'lora_up': lora_up}
    _L0_ffn_all = _L0_ffn_setup()
    _L0_ffn_in = {k: v for k, v in _L0_ffn_all.items() if k in ('router_w', 'lora_down', 'lora_up')}
    del _L0_ffn_all
    return {'x': x, 'ctx_1024': ctx_1024, 'mask_1x1xSxS2_bk0': mask_1x1xSxS2_bk0, 'L0_xattn_W_q': _L0_xattn_in['W_q'], 'L0_xattn_W_k': _L0_xattn_in['W_k'], 'L0_xattn_W_v': _L0_xattn_in['W_v'], 'L0_xattn_W_o': _L0_xattn_in['W_o'], 'L0_ffn_router_w': _L0_ffn_in['router_w'], 'L0_ffn_lora_down': _L0_ffn_in['lora_down'], 'L0_ffn_lora_up': _L0_ffn_in['lora_up']}

def reference(x, ctx_1024, mask_1x1xSxS2_bk0, L0_xattn_W_q, L0_xattn_W_k, L0_xattn_W_v, L0_xattn_W_o, L0_ffn_router_w, L0_ffn_lora_down, L0_ffn_lora_up):
    import jax
    import jax.numpy as jnp

    def _L0_xattn_ref(q, k, v, mask, W_q, W_k, W_v, W_o):
        import jax, jax.numpy as jnp
        import numpy as np
        D_MODEL = 256
        NUM_HEADS = 16
        HEAD_DIM = D_MODEL // NUM_HEADS
        B, S, _ = q.shape
        H, Dh = (NUM_HEADS, HEAD_DIM)

        def proj(x, W):
            return (x @ W.T).reshape(B, -1, H, Dh).transpose(0, 2, 1, 3)
        Q, K, V = (proj(q, W_q), proj(k, W_k), proj(v, W_v))
        scores = jnp.einsum('bhqd,bhkd->bhqk', Q, K) / np.sqrt(Dh)
        scores = jnp.where(mask, scores, -1000000000.0)
        attn = jax.nn.softmax(scores, axis=-1)
        out = jnp.einsum('bhqk,bhkd->bhqd', attn, V)
        out = out.transpose(0, 2, 1, 3).reshape(B, S, D_MODEL)
        return out @ W_o.T

    def _L0_ffn_ref(x, router_w, lora_down, lora_up):
        import jax, jax.numpy as jnp
        import numpy as np
        B, L, H = (32, 128, 256)
        E, R, TOP_K = (8, 16, 2)

        def _gates(cls, router_w):
            logits = jnp.einsum('bh,eh->be', cls, router_w)
            top_vals, top_idx = jax.lax.top_k(logits, TOP_K)
            mask = jnp.full_like(logits, -jnp.inf)
            rows = jnp.arange(logits.shape[0])[:, None]
            mask = mask.at[rows, top_idx].set(top_vals)
            return jax.nn.softmax(mask, axis=1)
        gates = _gates(x[:, 0, :], router_w)
        down = jnp.einsum('blh,erh->bler', x, lora_down)
        weighted = jnp.einsum('bler,ehr,be->blh', down, lora_up, gates)
        return x + weighted
    x = x + _L0_xattn_ref(_layernorm(x, axis=-1), ctx_1024, ctx_1024, mask_1x1xSxS2_bk0, L0_xattn_W_q, L0_xattn_W_k, L0_xattn_W_v, L0_xattn_W_o)
    x = x + _L0_ffn_ref(_layernorm(x, axis=-1), L0_ffn_router_w, L0_ffn_lora_down, L0_ffn_lora_up)
    return x

_drawn_inputs = setup_inputs


def setup_inputs(seed=0):
    import zlib

    import numpy as np

    out = dict(_drawn_inputs(seed))
    spreads = {}
    factors = {}
    for name, (base, spread) in spreads.items():
        noise = np.random.default_rng([zlib.crc32(name.encode()), seed]).standard_normal(out[name].shape)
        drawn = base * np.exp(spread * noise) if base else spread * noise
        out[name] = jnp.asarray(drawn.astype(out[name].dtype))
    for name, factor in factors.items():
        out[name] = (out[name] * factor).astype(out[name].dtype)
    return out
```

```python
from contextlib import ExitStack

import concourse.bass as bass
from concourse import mybir

F32 = mybir.dt.float32
BF16 = mybir.dt.bfloat16
F16 = mybir.dt.float16
U8 = mybir.dt.uint8
I32 = mybir.dt.int32
ALU = mybir.AluOpType
ACT = mybir.ActivationFunctionType
X = mybir.AxisListType.X

D, H, HD = 256, 16, 16
NB, S, SK = 4, 1024, 154
E, R = 8, 16
P = 128
QB = 512
NJ = QB // P
NBLK = NB * S // QB
KC = D // P
TAIL = SK - P
SKP = P + 32
SLOTQ = (0, 0, 0, 1, 1, 2)
SLOTK = (0, 1, 2, 0, 1, 0)
NROW = 16 * len(SLOTQ)
NMAX = NROW + 3
VW = 3 * HD + 1
HG = H // 2
VG = 2 * HG * VW
NT = 10
NK = 2 * NT
HPB = 3
NU = (H + HPB - 1) // HPB
MASKED = -float(2 ** 99)
SHIFT = 9.704060527839234
EPS = 1e-5
RSQRT_BITS = float(0x5F3759DF)
NEWTON = 3
SCALE = 0.25
POOL_TILES = (2, 5, 8, 12, 15, 18)


class Blk:

    def __init__(self, i, o):
        self.i, self.o, self.par = i, o, o % 2

    def at(self, d):
        return Blk(self.i, self.o + d)

    def row(self):
        return self.i * (2 * QB) + self.o * QB


def build(nc, x, ctxT, mask, maskT, wqT, wkT, wvT, woT, routerT, downT, upT, ident, tri, out):
    with ExitStack() as es:
        def sb(name, shape, dt=F32):
            return es.enter_context(nc.sbuf_tensor(name, shape, dt))

        def psum(name):
            return es.enter_context(nc.psum_tensor(name, [P, 512], F32))

        def sem(name):
            return es.enter_context(nc.semaphore(name))

        wq, wk, wv, wo = (sb(n, [P, KC, D]) for n in ("wq", "wk", "wv", "wo"))
        wdown = sb("wdown", [P, KC, E * R])
        wup = sb("wup", [P, D])
        wrout = sb("wrout", [P, KC, E])
        id32 = sb("id32", [P, P])
        id16 = sb("id16", [P, P], BF16)
        tri_sb = sb("tri_sb", [1, E * E])
        one1 = sb("one1", [1, 1])
        m8 = sb("m8", [P, S // P, SK], U8)
        mt8 = sb("mt8", [P, S], U8)
        mtt8 = sb("mtt8", [P, S], U8)
        maskq = sb("maskq", [P, S // P, SK], BF16)
        maskk = sb("maskk", [P, S], BF16)
        maskt = sb("maskt", [P, S], BF16)
        cin = sb("cin", [P, KC, SK])
        ctail = sb("ctail", [P, KC, 4, 32])
        kp = sb("kp", [P, 3, 2, SKP], BF16)
        kr = sb("kr", [P, 2, SK])
        kst_n = sb("kst_n", [NMAX, H, SKP], BF16)
        kst_c = sb("kst_c", [NMAX, H, SKP], BF16)
        v_n = sb("v_n", [P, 2, VG], BF16)
        v_c = sb("v_c", [P, 2, VG], BF16)
        vr = sb("vr", [P, 2, D])
        kdram = nc.dram_tensor("kdram", [P, 3, 2, SKP], BF16).ap()
        xin = [sb(f"xin{s}", [P, NJ, D]) for s in range(2)]
        xres = [sb(f"xres{s}", [P, NJ, D]) for s in range(2)]
        stats = sb("stats", [P, NJ, 6])
        mv = sb("mv", [P, NJ, 2])
        rstd = sb("rstd", [P, NJ])
        nmr = sb("nmr", [P, NJ])
        stats2 = sb("stats2", [P, NJ, 6])
        mv2 = sb("mv2", [P, NJ, 2])
        rstd2 = sb("rstd2", [P, NJ])
        nmr2 = sb("nmr2", [P, NJ])
        var = sb("var", [P, NJ])
        var2 = sb("var2", [P, NJ])
        newt = sb("newt", [P, NJ])
        xn = sb("xn", [P, NJ, D])
        xnT = sb("xnT", [P, KC, QB])
        qp = sb("qp", [P, 3, 2, QB], BF16)
        qr = sb("qr", [P, 2, QB])
        qst = [sb(f"qst{s}", [NMAX, H, QB], BF16) for s in range(2)]
        negm = sb("negm", [P, NJ, H])
        nms = sb("nms", [P, NJ, H])
        nmp = sb("nmp", [P, NJ, 3, H], BF16)
        nmr1 = sb("nmr1", [P, NJ, H])
        nmT = sb("nmT", [3 * H, QB], BF16)
        p32 = sb("p32", [P, 2, QB])
        pa = [sb(f"pa{g}", [P, NT, QB], F16) for g in range(2)]
        pb = [sb(f"pb{g}", [P, NT, QB], F16) for g in range(2)]
        osum = sb("osum", [P, 2, HG, HD])
        rden = sb("rden", [P, 2, HG])
        on = sb("on", [P, NJ, D])
        oT = sb("oT", [P, KC, QB])
        x1 = sb("x1", [P, NJ, D])
        x2 = sb("x2", [P, NJ, D])
        z = sb("z", [P, NJ, D])
        x2T = sb("x2T", [P, KC, QB])
        dn = sb("dn", [P, QB])
        y = sb("y", [P, NJ, D])
        g_l = sb("g_l", [1, E])
        g_eq = sb("g_eq", [1, E, E])
        g_gt = sb("g_gt", [1, E, E])
        g_sel = sb("g_sel", [1, 8, E])
        g_s = sb("g_s", [1, 4])
        g_row = sb("g_row", [1, E, R])
        g_col = sb("g_col", [P, 1])

        ps_s = [psum(f"ps_s{k}") for k in range(2)]
        ps_t = [psum(f"ps_t{k}") for k in range(2)]
        ps_o = [psum(f"ps_o{k}") for k in range(2)]
        ps_d = [psum(f"ps_d{k}") for k in range(2)]

        passed = sem("passed")
        consts_in = sem("consts_in")
        late_consts_in = sem("late_consts_in")
        masks_in = sem("masks_in")
        pool_cleared = sem("pool_cleared")
        dve_cleared = sem("dve_cleared")
        id16_ready = sem("id16_ready")
        masks_ready = sem("masks_ready")
        ctx_in = sem("ctx_in")
        tail_copied = sem("tail_copied")
        x_in = [sem(f"x_in{s}") for s in range(2)]
        xres_in = [sem(f"xres_in{s}") for s in range(2)]
        dve_step = sem("dve_step")
        act_step = sem("act_step")
        pool_step = sem("pool_step")
        d_full = [sem(f"d_full{k}") for k in range(2)]
        d_free = [sem(f"d_free{k}") for k in range(2)]
        ln1_stats = sem("ln1_stats")
        ln1_scale = sem("ln1_scale")
        ln2_scale = sem("ln2_scale")
        xn_ready = sem("xn_ready")
        q1_ready = sem("q1_ready")
        qr_ready = sem("qr_ready")
        q2_ready = sem("q2_ready")
        q3_ready = sem("q3_ready")
        q_heads = [[sem(f"q_heads{s}{g}") for g in range(2)] for s in range(2)]
        q_stack = [[sem(f"q_stack{s}{g}") for g in range(2)] for s in range(2)]
        v_zero = sem("v_zero")
        k1_ready = sem("k1_ready")
        kr_ready = sem("kr_ready")
        k2_ready = sem("k2_ready")
        k3_ready = sem("k3_ready")
        k_dram = sem("k_dram")
        kst_n_in = sem("kst_n_in")
        kst_c_in = [sem(f"kst_c_in{g}") for g in range(2)]
        v1_ready = sem("v1_ready")
        vr_ready = sem("vr_ready")
        v2_ready = sem("v2_ready")
        v3_ready = sem("v3_ready")
        v_c_in = [sem(f"v_c_in{g}") for g in range(2)]
        s_full = sem("s_full")
        s_free = sem("s_free")
        nmp_ready = sem("nmp_ready")
        nm_rows = [sem(f"nm_rows{s}") for s in range(2)]
        t_full = sem("t_full")
        t_done = sem("t_done")
        pb_dve = sem("pb_dve")
        pb_pool = sem("pb_pool")
        o_full = sem("o_full")
        o_free = sem("o_free")
        on_ready = sem("on_ready")
        x1_ready = sem("x1_ready")
        ln2_stats = sem("ln2_stats")
        x2_ready = sem("x2_ready")
        z_ready = sem("z_ready")
        g_diff = sem("g_diff")
        g_exp = sem("g_exp")
        g_row_ready = sem("g_row_ready")
        one_ready = sem("one_ready")
        g_col_ready = sem("g_col_ready")
        y_ready = sem("y_ready")
        y_out = sem("y_out")

        def val(b, f):
            if isinstance(b.i, int):
                return f(2 * b.i + b.o)
            at1, at2 = f(2 + b.o), f(4 + b.o)
            return b.i * (at2 - at1) + (2 * at1 - at2)

        def wait(eng, s, v):
            if not isinstance(v, int) or v > 0:
                eng.wait_ge(s, v)

        def hold(eng, s, v):
            wait(eng, s, v)
            eng.sem_inc(passed, 1)

        uses = []

        def use(name, t, bank):
            uses.append((name, t, bank))

        def plan_kv(b):
            for n, k in (("k0", 0), ("k1", 1), ("v0", 0), ("v1", 1)):
                use(n, 2 * b, k)

        def plan_project(t):
            for n, k in (("xT0", 0), ("xT1", 1), ("q0", 0), ("q1", 1)):
                use(n, t, k)

        def plan_finish(t, part):
            if part == 0:
                for n, k in (("oT0", 0), ("oT1", 1), ("wo0", 0), ("wo1", 1)):
                    use(n, t, k)
                return
            use("x2T0", t, 0)
            use("x2T1", t, 1)
            if t % 2 == 0:
                use("logit", t, 0)
                use("gcol", t, 1)
            use("down", t, 0)
            use("up0", t, 1)
            use("up1", t, 0)

        plan_kv(0)
        plan_project(0)
        plan_project(1)
        use("nmT", 0, 1)
        for t in range(NBLK):
            if t % 2 == 0 and t + 2 < NBLK:
                plan_kv(t // 2 + 1)
            if t > 0:
                plan_finish(t - 1, 0)
            if t + 2 < NBLK:
                plan_project(t + 2)
            if t > 0:
                plan_finish(t - 1, 1)
            if t + 1 < NBLK:
                use("nmT", t + 1, 1)
        plan_finish(NBLK - 1, 0)
        plan_finish(NBLK - 1, 1)
        ordinal, bank_of, seen = {}, {}, [0, 0]
        for n, t, k in uses:
            seen[k] += 1
            ordinal[n, t] = seen[k]
            bank_of[n] = k

        def nth(b, name):
            return val(b, lambda t: ordinal[name, t])

        def fill(pe, b, name):
            k = bank_of[name]
            wait(pe, d_free[k], val(b, lambda t: ordinal[name, t] - 1))
            return ps_d[k]

        def full(eng, b, name):
            k = bank_of[name]
            eng.wait_ge(d_full[k], nth(b, name))
            return ps_d[k]

        def pb_count(n, on_pool):
            whole, rest = divmod(n, NK)
            mine = [k for k in range(NK) if (k in POOL_TILES) == on_pool]
            return whole * len(mine) + sum(k < rest for k in mine)

        def tile_of(k):
            g, kk = divmod(k, NT)
            return g, kk, kk // 5, kk % 5

        class Slot:
            def __init__(self, b, first, last):
                self.b = b
                self.has_finish = not (first and b.par == 0)
                self.has_project = not last
                self.has_maxima = not (last and b.par == 1)
                self.has_kv = not last and b.par == 0
                self.nxt, self.prj, self.fin = b.at(1), b.at(2), b.at(-1)

        def run(eng, slot):
            for s in range(2):
                slot(Slot(Blk(0, s), True, False))
            with eng.Fori(1, NB - 1) as i:
                for s in range(2):
                    slot(Slot(Blk(i, s), False, False))
            for s in range(2):
                slot(Slot(Blk(NB - 1, s), False, True))

        UNITS = [(kb, j) for kb in range(NU) for j in range(NJ)]

        def units_at(k):
            return UNITS[2 * (k - 6):2 * (k - 6) + 2] if 6 <= k < 18 else []

        block = es.enter_context(nc.Block())

        @block.sync
        def _(sp):
            def load_ctx(b):
                hold(sp, d_full[1], val(b, lambda t: ordinal["v1", t - 2] if t >= 2 else 0))
                hold(sp, tail_copied, val(b, lambda t: t // 2))
                bi = b.i + b.o // 2
                src = ctxT[bi:bi + 1] if isinstance(bi, int) else ctxT[bass.ds(bi, 1)]
                sp.dma_start(cin[:], src.rearrange("a (c p) k -> p (a c) k", p=P)).then_inc(ctx_in, 16)

            def load_x(b):
                hold(sp, xn_ready, val(b, lambda t: NJ * (t - 1)))
                sp.dma_start(xin[b.par][:], x[bass.ds(b.row(), QB), :].rearrange("(j p) d -> p j d", p=P)
                             ).then_inc(x_in[b.par], 16)

            def load_xres(b):
                hold(sp, x1_ready, val(b, lambda t: 2 * (t - 1)))
                sp.dma_start(xres[b.par][:], x[bass.ds(b.row(), QB), :].rearrange("(j p) d -> p j d", p=P)
                             ).then_inc(xres_in[b.par], 16)

            def stack_q(b, g):
                s = b.par
                hold(sp, q3_ready, val(b, lambda t: 2 * (t + 1)))
                hold(sp, t_full, val(b, lambda t: NK * (t - 2) + NT * (g + 1) if t >= 2 else 0))
                for hh in range(4 * g, 4 * g + 4):
                    for part, slot in ((0, 0), (1, 3), (2, 5)):
                        sp.dma_start(qst[s][16 * slot:16 * slot + 16, 2 * hh:2 * hh + 2, :],
                                     qp[16 * hh:16 * hh + 16, part, :, :]).then_inc(q_heads[s][g], 16)
                hold(sp, q_heads[s][g], val(b, lambda t: 16 * 12 * (t // 2 + 1)))
                for frm, to in ((0, 1), (0, 2), (3, 4)):
                    sp.dma_start(qst[s][16 * to:16 * to + 16, HG * g:HG * g + HG, :],
                                 qst[s][16 * frm:16 * frm + 16, HG * g:HG * g + HG, :]
                                 ).then_inc(q_stack[s][g], 16)

            def stack_k(b):
                hold(sp, k3_ready, val(b, lambda t: 2 * (t // 2 + 1)))
                sp.dma_start(kdram, kp[:]).then_inc(k_dram, 16)
                hold(sp, s_full, val(b, lambda t: len(UNITS) * t))
                for g in range(2):
                    hold(sp, kst_c_in[g], val(b, lambda t: 16 * (t // 2)))
                hold(sp, k_dram, val(b, lambda t: 16 * (t // 2 + 1)))
                for slot, part in enumerate(SLOTK):
                    sp.dma_start(kst_n[16 * slot:16 * slot + 16].rearrange("d (hh m) k -> d hh m k", m=2),
                                 kdram[:, part].rearrange("(hh d) m k -> d hh m k", d=16)
                                 ).then_inc(kst_n_in, 16)

            def keys_to_attend(b, g):
                hold(sp, kst_n_in, val(b, lambda t: 16 * 6 * (t // 2 + 1)))
                hold(sp, t_full, val(b, lambda t: NK * (t - 1) + NT * (g + 1) if t else 0))
                sp.dma_start(kst_c[:, HG * g:HG * g + HG, :], kst_n[:, HG * g:HG * g + HG, :]
                             ).then_inc(kst_c_in[g], 16)
                hold(sp, v3_ready, val(b, lambda t: 5 * (t // 2 + 1)))
                hold(sp, o_full, val(b, lambda t: 2 * NJ * (t - 1) + NJ * (g + 1) if t else 0))
                sp.dma_start(v_c[:, g, :], v_n[:, g, :]).then_inc(v_c_in[g], 16)

            def max_rows(b):
                hold(sp, d_free[1], nth(b, "nmT"))
                for part in range(3):
                    sp.dma_start(qst[b.par][NROW + part:NROW + part + 1, :, :],
                                 nmT[16 * part:16 * part + 16, :]).then_inc(nm_rows[b.par], 16)

            b0 = Blk(0, 0)
            load_x(b0)
            load_ctx(b0)
            sp.dma_start(wk[:], wkT.rearrange("(c p) n -> p c n", p=P)).then_inc(consts_in, 16)
            sp.dma_start(id32[:], ident).then_inc(consts_in, 16)
            sp.dma_start(wq[:], wqT.rearrange("(c p) n -> p c n", p=P)).then_inc(consts_in, 16)
            sp.dma_start(wv[:], wvT.rearrange("(c p) n -> p c n", p=P)).then_inc(consts_in, 16)
            load_x(b0.at(1))
            sp.wait_ge(pool_cleared, 1)
            sp.dma_start(m8[:], mask.rearrange("(j p) k -> p j k", p=P)).then_inc(masks_in, 16)
            sp.dma_start(mt8[:], maskT[0:P, :]).then_inc(masks_in, 16)
            for q in range(4):
                sp.dma_start(mtt8[32 * q:32 * q + TAIL, :], maskT[P:SK, :]).then_inc(masks_in, 16)
            sp.wait_ge(dve_cleared, 3)
            stack_k(b0)
            for g in range(2):
                keys_to_attend(b0, g)
            for g in range(2):
                stack_q(b0, g)
            sp.dma_start(wo[:], woT.rearrange("(c p) n -> p c n", p=P)).then_inc(late_consts_in, 16)
            sp.dma_start(wdown[:], downT.rearrange("(c p) n -> p c n", p=P)).then_inc(late_consts_in, 16)
            sp.dma_start(wup[:], upT).then_inc(late_consts_in, 16)
            sp.dma_start(wrout[:], routerT.rearrange("(c p) n -> p c n", p=P)).then_inc(late_consts_in, 16)
            sp.dma_start(tri_sb[:], tri).then_inc(late_consts_in, 16)
            for g in range(2):
                stack_q(b0.at(1), g)
            max_rows(b0)

            def slot(sl):
                b = sl.b
                load_xres(b)
                if sl.has_kv:
                    load_ctx(b.at(2))
                if sl.has_project and b.par == 0:
                    load_x(b.at(2))
                    load_x(b.at(3))
                if sl.has_project:
                    stack_q(sl.prj, 0)
                if b.par == 1 and sl.has_project:
                    keys_to_attend(b.at(1), 0)
                if sl.has_maxima:
                    max_rows(sl.nxt)
                if sl.has_kv:
                    stack_k(b.at(2))
                if sl.has_project:
                    stack_q(sl.prj, 1)
                if b.par == 1 and sl.has_project:
                    keys_to_attend(b.at(1), 1)

            run(sp, slot)
            sp.wait_ge(y_out, 16 * NBLK)

        @block.gpsimd
        def _(pool):
            order = [("ln1", 0), ("ln1", 1)]
            for t in range(NBLK):
                order += [("ln1", t + 2)] * (t + 2 < NBLK) + [("ln2", t - 1)] * (t > 0)
            order.append(("ln2", NBLK - 1))
            steps_of_norm = 4 * NEWTON + 1

            def scales(b, name, mv, var, rstd, nmr, stats_ready, ready):
                pool.wait_ge(stats_ready, val(b, lambda t: t + 1))
                n = 0
                for _ in range(NEWTON):
                    for what in range(4):
                        if what == 0:
                            ins = pool.tensor_tensor(newt[:], rstd[:], rstd[:], ALU.mult)
                        elif what == 1:
                            ins = pool.tensor_tensor(newt[:], newt[:], var[:], ALU.mult)
                        elif what == 2:
                            ins = pool.tensor_scalar(newt[:], newt[:], -0.5, 1.5, ALU.mult, ALU.add)
                        else:
                            ins = pool.tensor_tensor(rstd[:], rstd[:], newt[:], ALU.mult)
                        n += 1
                        ins.then_inc(pool_step, 1)
                        hold(pool, pool_step, val(b, lambda t: 1 + steps_of_norm * order.index((name, t)) + n))
                pool.tensor_tensor(nmr[:], mv[:, :, 0], rstd[:], ALU.mult).then_inc(pool_step, 1)
                hold(pool, pool_step, val(b, lambda t: 1 + steps_of_norm * order.index((name, t)) + n + 1))
                pool.tensor_scalar(nmr[:], nmr[:], -1.0, None, ALU.mult).then_inc(ready, 1)

            def scales1(b):
                scales(b, "ln1", mv, var, rstd, nmr, ln1_stats, ln1_scale)

            def scales2(b):
                scales(b, "ln2", mv2, var2, rstd2, nmr2, ln2_stats, ln2_scale)

            def copy_tail(b):
                pool.wait_ge(ctx_in, val(b, lambda t: 16 * (t // 2 + 1)))
                hold(pool, d_full[1], val(b, lambda t: ordinal["v1", t - 2] if t >= 2 else 0))
                for c in range(KC):
                    ins = pool.tensor_copy(ctail[:, c, :, 0:TAIL],
                                           cin[:, c, P:SK].unsqueeze(1).broadcast_to([P, 4, TAIL]))
                ins.then_inc(tail_copied, 1)

            def residual(b, k):
                g, kk, _, _ = tile_of(k)
                pool.wait_ge(t_done, val(b, lambda t: NK * t + k + 1))
                wait(pool, o_full, val(b, lambda t: 2 * NJ * (t - 1) + NJ * (g + 1) if t else 0))
                pool.tensor_tensor(pb[g][:, kk, :], p32[:, k % 2, :], pa[g][:, kk, :],
                                   ALU.subtract).then_inc(pb_pool, 1)

            def normalise(b, g, j):
                pool.wait_ge(o_free, val(b, lambda t: 2 * NJ * t + NJ * g + j + 1))
                if g == 0 and j == 0:
                    wait(pool, d_full[1], val(b, lambda t: ordinal["oT1", t - 1] if t else 0))
                pool.tensor_tensor(on[:, j, P * g:P * g + P].rearrange("p (h d) -> p h d", d=HD),
                                   osum[:, j % 2], rden[:, j % 2].unsqueeze(2).broadcast_to([P, HG, HD]),
                                   ALU.mult).then_inc(on_ready, 1)

            def add_norms(b):
                pool.wait_ge(x2_ready, val(b, lambda t: NJ * (t + 1)))
                wait(pool, y_ready, val(b, lambda t: 2 * t))
                pool.tensor_tensor(z[:], x1[:], x2[:], ALU.add).then_inc(z_ready, 1)

            pool.memset(mtt8[:], 0).then_inc(pool_cleared, 1)
            pool.memset(kp[:], 0.0).then_inc(pool_cleared, 1)
            pool.memset(ctail[:], 0.0).then_inc(pool_step, 1)
            pool.wait_ge(pool_step, 1)
            scales1(Blk(0, 0))
            copy_tail(Blk(0, 0))
            scales1(Blk(0, 1))

            def slot(sl):
                for k in range(NK):
                    if k == 3 and sl.has_project:
                        scales1(sl.prj)
                    if k == 6 and sl.has_finish:
                        scales2(sl.fin)
                    if k == 1 and sl.has_kv:
                        copy_tail(sl.b.at(2))
                    if k in POOL_TILES:
                        residual(sl.b, k)
                    if k == 8 and sl.has_finish:
                        add_norms(sl.fin)
                    if 12 <= k < 16:
                        normalise(sl.b, 0, k - 12)
                for j in range(NJ):
                    normalise(sl.b, 1, j)

            run(pool, slot)
            scales2(Blk(NB, -1))
            add_norms(Blk(NB, -1))

        @block.scalar
        def _(act):
            def exps(b, k):
                g, kk, _, _ = tile_of(k)
                act.wait_ge(t_full, val(b, lambda t: NK * t + k + 1))
                engine_has = (k - 2) % NK in POOL_TILES
                wait(act, pb_pool if engine_has else pb_dve,
                     val(b, lambda t: pb_count(NK * t + k - 1, engine_has) if NK * t + k >= 2 else 0))
                act.activation(p32[:, k % 2, :], ps_t[k % 2][:], ACT.Exp)
                if kk == 0:
                    wait(act, o_full, val(b, lambda t: 2 * NJ * (t - 1) + NJ * (g + 1) if t else 0))
                act.activation(pa[g][:, kk, :], ps_t[k % 2][:], ACT.Exp).then_inc(t_done, 1)

            def norm1(b):
                act.wait_ge(ln1_scale, val(b, lambda t: t + 1))
                wait(act, d_full[1], val(b, lambda t: ordinal["xT1", t - 1] if t else 0))
                for j in range(NJ):
                    act.activation(xn[:, j, :], xin[b.par][:, j, :], ACT.Identity, bias=nmr[:, j:j + 1],
                                   scale=rstd[:, j:j + 1]).then_inc(xn_ready, 1)

            def norm2(b):
                act.wait_ge(ln2_scale, val(b, lambda t: t + 1))
                wait(act, d_full[1], val(b, lambda t: ordinal["x2T1", t - 1] if t else 0))
                wait(act, z_ready, val(b, lambda t: t))
                for j in range(NJ):
                    act.activation(x2[:, j, :], x1[:, j, :], ACT.Identity, bias=nmr2[:, j:j + 1],
                                   scale=rstd2[:, j:j + 1]).then_inc(x2_ready, 1)

            def xT(b):
                for c in range(KC):
                    src = full(act, b, f"xT{c}")
                    if c == 0:
                        wait(act, d_full[1], val(b, lambda t: ordinal["q1", t - 1] if t else 0))
                    act.copy(xnT[:, c, :], src[:]).then_inc(d_free[c], 1)

            def q1(b):
                for m in range(2):
                    src = full(act, b, f"q{m}")
                    if m == 0:
                        for g in range(2):
                            wait(act, q_heads[(b.par + 1) % 2][g],
                                 val(b, lambda t: 16 * 12 * ((t - 1) // 2 + 1) if t else 0))
                    act.activation(qp[:, 0, m, :], src[:], ACT.Copy, scale=SCALE).then_inc(q1_ready, 1)

            def q2(b):
                for m in range(2):
                    act.wait_ge(qr_ready, val(b, lambda t: 2 * t + m + 1))
                    act.copy(qp[:, 1, m, :], qr[:, m, :]).then_inc(q2_ready, 1)

            def k1(b):
                for m in range(2):
                    src = full(act, b, f"k{m}")
                    if m == 0:
                        wait(act, k_dram, val(b, lambda t: 16 * (t // 2)))
                        if isinstance(b.i, int) and b.i == 0 and b.o == 0:
                            act.wait_ge(pool_cleared, 2)
                    act.copy(kp[:, 0, m, 0:SK], src[:, 0:SK]).then_inc(k1_ready, 1)

            def k2(b):
                for m in range(2):
                    act.wait_ge(kr_ready, val(b, lambda t: 2 * (t // 2) + m + 1))
                    act.copy(kp[:, 1, m, 0:SK], kr[:, m, :]).then_inc(k2_ready, 1)

            def v_main(part):
                v = v_n[:].rearrange("p g (h e) -> p g h e", e=VW)
                return v[:, :, 0:HG, HD * part:HD * part + HD]

            def v1(b):
                src = full(act, b, "v0")
                for g in range(2):
                    wait(act, v_c_in[g], val(b, lambda t: 16 * (t // 2)))
                if isinstance(b.i, int) and b.i == 0 and b.o == 0:
                    act.wait_ge(dve_cleared, 2)
                for g in range(2):
                    ins = act.copy(v_main(0)[:, g], src[:, P * g:P * g + P].rearrange("p (h d) -> p h d", d=HD))
                ins.then_inc(v1_ready, 1)
                src = full(act, b, "v1")
                for q in range(4):
                    rows = slice(32 * q, 32 * q + 32)
                    ins = act.copy(v_tail(q, 0), vt_in(src[rows, 0:D], q))
                ins.then_inc(v1_ready, 1)

            def vt_in(a, q):
                return a.rearrange("p (gg h d) -> p gg h d", gg=4, d=HD)[:, :, q, :]

            def v_tail(q, part):
                v = v_n[32 * q:32 * q + 32].rearrange("p g (a gg h e) -> p g a gg h e", a=2, gg=2, e=VW)
                return v[:, :, 1, :, q, HD * part:HD * part + HD]

            def v2(b):
                act.wait_ge(vr_ready, val(b, lambda t: 2 * (t // 2) + 1))
                for g in range(2):
                    ins = act.copy(v_main(1)[:, g], vr[:, 0, P * g:P * g + P].rearrange("p (h d) -> p h d", d=HD))
                ins.then_inc(v2_ready, 1)
                act.wait_ge(vr_ready, val(b, lambda t: 2 * (t // 2) + 2))
                for q in range(4):
                    ins = act.copy(v_tail(q, 1), vt_in(vr[32 * q:32 * q + 32, 1, :], q))
                ins.then_inc(v2_ready, 1)

            def nm_out(b):
                src = full(act, b, "nmT")
                wait(act, nm_rows[(b.par + 1) % 2], val(b, lambda t: 48 * ((t - 1) // 2 + 1) if t else 0))
                act.copy(nmT[:], src[0:3 * H, 0:QB // 2].bitcast(BF16)).then_inc(d_free[1], 1)

            def oT_out(b):
                for c in range(KC):
                    src = full(act, b, f"oT{c}")
                    if c == 0:
                        wait(act, d_full[1], val(b, lambda t: ordinal["wo1", t - 1] if t else 0))
                    act.copy(oT[:, c, :], src[:]).then_inc(d_free[c], 1)

            def x2T_out(b):
                for c in range(KC):
                    src = full(act, b, f"x2T{c}")
                    if c == 0:
                        wait(act, d_full[0], val(b, lambda t: ordinal["down", t - 1] if t else 0))
                    act.copy(x2T[:, c, :], src[:]).then_inc(d_free[c], 1)

            def gate_exp(b):
                act.wait_ge(g_diff, val(b, lambda t: t // 2 + 1))
                act.activation(g_sel[:, 2, :], g_sel[:, 1, :], ACT.Exp).then_inc(g_exp, 1)

            def dn_out(b):
                src = full(act, b, "down")
                act.wait_ge(g_col_ready, val(b, lambda t: t // 2 + 1))
                wait(act, d_full[0], val(b, lambda t: ordinal["up1", t - 1] if t else 0))
                act.activation(dn[:], src[:], ACT.Copy, scale=g_col[:, 0:1]).then_inc(d_free[0], 1)

            def store(b):
                act.wait_ge(y_ready, val(b, lambda t: 2 * (t + 1)))
                act.dma_start(out[bass.ds(b.row(), QB), :].rearrange("(j p) d -> p j d", p=P), y[:]
                              ).then_inc(y_out, 16)

            b0 = Blk(0, 0)
            norm1(b0)
            k1(b0)
            k2(b0)
            v1(b0)
            v2(b0)
            xT(b0)
            q1(b0)
            q2(b0)
            norm1(b0.at(1))
            xT(b0.at(1))
            q1(b0.at(1))
            q2(b0.at(1))
            nm_out(b0)

            def slot(sl):
                for k in range(NK):
                    exps(sl.b, k)
                    if k == 1 and sl.has_kv:
                        k1(sl.b.at(2))
                    if k == 2 and sl.has_kv:
                        k2(sl.b.at(2))
                        v1(sl.b.at(2))
                    if k == 3 and sl.has_kv:
                        v2(sl.b.at(2))
                    if k == 3 and sl.has_project:
                        norm1(sl.prj)
                    if k == 3 and sl.has_finish:
                        oT_out(sl.fin)
                    if k == 6 and sl.has_project:
                        xT(sl.prj)
                    if k == 7 and sl.has_project:
                        q1(sl.prj)
                    if k == 7 and sl.has_finish:
                        norm2(sl.fin)
                    if k == 8 and sl.has_project:
                        q2(sl.prj)
                    if k == 9 and sl.has_finish:
                        x2T_out(sl.fin)
                    if k == 11 and sl.has_finish and sl.fin.par == 0:
                        gate_exp(sl.fin)
                    if k == 13 and sl.has_finish:
                        dn_out(sl.fin)
                    if k == 16 and sl.has_finish:
                        store(sl.fin)
                if sl.has_maxima:
                    nm_out(sl.nxt)

            run(act, slot)
            last = Blk(NB, -1)
            oT_out(last)
            norm2(last)
            x2T_out(last)
            dn_out(last)
            store(last)

        @block.vector
        def _(dve):
            order, done = [], {}
            STEPS = {"ln1": 2 * NJ + 2, "ln2": 2 * NJ + 2, "parts": 4, "gate_a": 8, "gate_b": 3}

            def plan(name, t):
                order.append((name, t))

            plan("ln1", 0)
            plan("ln1", 1)
            plan("parts", 0)
            for t in range(NBLK):
                if t + 2 < NBLK:
                    plan("ln1", t + 2)
                if t > 0:
                    plan("ln2", t - 1)
                    if (t - 1) % 2 == 0:
                        plan("gate_a", t - 1)
                        plan("gate_b", t - 1)
                if t + 1 < NBLK:
                    plan("parts", t + 1)
            plan("ln2", NBLK - 1)
            total = 0
            for key in order:
                done[key] = total
                total += STEPS[key[0]]

            def step(ins, b, name, n):
                ins.then_inc(dve_step, 1)
                if name in ("ln1", "ln2"):
                    hold(dve, dve_step, val(b, lambda t: done[name, t] + n))
                else:
                    dve.wait_ge(dve_step, val(b, lambda t: done[name, t] + n))

            def mark(ins):
                ins.then_inc(dve_step, 1)

            def layer_stats(b, name, src, stats, mv, var, rstd, ready):
                for j in range(NJ):
                    ins = dve.bn_stats(stats[:, j, :], src[:, j, :])
                    mark(ins) if j < NJ - 1 else step(ins, b, name, NJ)
                for j in range(NJ):
                    ins = dve.bn_aggr(mv[:, j, :], stats[:, j, :])
                    mark(ins) if j < NJ - 1 else step(ins, b, name, 2 * NJ)
                step(dve.tensor_scalar(var[:], mv[:, :, 1], EPS, None, ALU.add), b, name, 2 * NJ + 1)
                step(dve.tensor_single_scalar(rstd[:].bitcast(I32), var[:].bitcast(I32), 1,
                                              ALU.logical_shift_right), b, name, 2 * NJ + 2)
                dve.tensor_scalar(rstd[:].bitcast(I32), rstd[:].bitcast(I32), -1.0, RSQRT_BITS, ALU.mult, ALU.add
                                  ).then_inc(ready, 1)

            def ln1(b):
                dve.wait_ge(x_in[b.par], val(b, lambda t: 16 * (t // 2 + 1)))
                wait(dve, xn_ready, val(b, lambda t: NJ * t))
                layer_stats(b, "ln1", xin[b.par], stats, mv, var, rstd, ln1_stats)

            def ln2(b):
                wait(dve, x2_ready, val(b, lambda t: NJ * t))
                dve.wait_ge(x1_ready, val(b, lambda t: 2 * (t + 1)))
                layer_stats(b, "ln2", x1, stats2, mv2, var2, rstd2, ln2_stats)

            def q_rest(b):
                for m in range(2):
                    dve.wait_ge(q1_ready, val(b, lambda t: 2 * t + m + 1))
                    wait(dve, q3_ready, val(b, lambda t: 2 * t))
                    wait(dve, q2_ready, val(b, lambda t: 2 * t))
                    dve.scalar_tensor_tensor(qr[:, m, :], ps_d[m][:], SCALE, qp[:, 0, m, :], ALU.mult,
                                             ALU.subtract).then_inc(qr_ready, 1)
                    dve.wait_ge(qr_ready, val(b, lambda t: 2 * t + m + 1))
                    dve.sem_inc(d_free[m], 1)

            def q3(b):
                for m in range(2):
                    dve.wait_ge(q2_ready, val(b, lambda t: 2 * t + m + 1))
                    dve.tensor_tensor(qp[:, 2, m, :], qr[:, m, :], qp[:, 1, m, :], ALU.subtract
                                      ).then_inc(q3_ready, 1)

            def k_rest(b):
                for m in range(2):
                    dve.wait_ge(k1_ready, val(b, lambda t: 2 * (t // 2) + m + 1))
                    wait(dve, k3_ready, val(b, lambda t: 2 * (t // 2)))
                    dve.tensor_tensor(kr[:, m, :], ps_d[m][:, 0:SK], kp[:, 0, m, 0:SK], ALU.subtract
                                      ).then_inc(kr_ready, 1)
                    dve.wait_ge(kr_ready, val(b, lambda t: 2 * (t // 2) + m + 1))
                    dve.sem_inc(d_free[m], 1)

            def k3(b):
                for m in range(2):
                    dve.wait_ge(k2_ready, val(b, lambda t: 2 * (t // 2) + m + 1))
                    dve.tensor_tensor(kp[:, 2, m, 0:SK], kr[:, m, :], kp[:, 1, m, 0:SK], ALU.subtract
                                      ).then_inc(k3_ready, 1)

            def heads(a):
                return a.rearrange("p (h d) -> p h d", d=HD)

            def v_main(g, part):
                return v_n[:, g, 0:HG * VW].rearrange("p (h e) -> p h e", e=VW)[:, :, HD * part:HD * part + HD]

            def v_tail(q, part):
                v = v_n[32 * q:32 * q + 32].rearrange("p g (a gg h e) -> p g a gg h e", a=2, gg=2, e=VW)
                return v[:, :, 1, :, q, HD * part:HD * part + HD]

            def vt_in(a, q):
                return a.rearrange("p (g gg h d) -> p g gg h d", g=2, gg=2, d=HD)[:, :, :, q, :]

            def v_rest(b):
                dve.wait_ge(v1_ready, val(b, lambda t: 2 * (t // 2) + 1))
                for g in range(2):
                    ins = dve.tensor_tensor(heads(vr[:, 0, P * g:P * g + P]), heads(ps_d[0][:, P * g:P * g + P]),
                                            v_main(g, 0), ALU.subtract)
                ins.then_inc(vr_ready, 1)
                dve.wait_ge(v1_ready, val(b, lambda t: 2 * (t // 2) + 2))
                for q in range(4):
                    r = slice(32 * q, 32 * q + 32)
                    ins = dve.tensor_tensor(vt_in(vr[r, 1, :], q), vt_in(ps_d[1][r, 0:D], q), v_tail(q, 0),
                                            ALU.subtract)
                ins.then_inc(vr_ready, 1)
                dve.wait_ge(vr_ready, val(b, lambda t: 2 * (t // 2) + 2))
                dve.sem_inc(d_free[0], 1)
                dve.sem_inc(d_free[1], 1)

            def v3(b):
                dve.wait_ge(v2_ready, val(b, lambda t: 2 * (t // 2) + 1))
                for g in range(2):
                    ins = dve.tensor_tensor(v_main(g, 2), heads(vr[:, 0, P * g:P * g + P]), v_main(g, 1),
                                            ALU.subtract)
                ins.then_inc(v3_ready, 1)
                dve.wait_ge(v2_ready, val(b, lambda t: 2 * (t // 2) + 2))
                for q in range(4):
                    dve.tensor_tensor(v_tail(q, 2), vt_in(vr[32 * q:32 * q + 32, 1, :], q), v_tail(q, 1),
                                      ALU.subtract).then_inc(v3_ready, 1)

            def maxima(b, u):
                kb, j = UNITS[u]
                n = min(HPB, H - HPB * kb)
                dve.wait_ge(s_full, val(b, lambda t: len(UNITS) * t + u + 1))
                dve.tensor_reduce(negm[:, j, HPB * kb:HPB * kb + n],
                                  ps_s[u % 2][:, 0:n * SK].rearrange("p (h k) -> p h k", k=SK),
                                  X, ALU.max, negate=True).then_inc(s_free, 1)

            def max_parts(b):
                dve.wait_ge(s_free, val(b, lambda t: len(UNITS) * (t + 1)))
                wait(dve, d_full[1], val(b, lambda t: ordinal["nmT", t - 1] if t else 0))
                step(dve.tensor_scalar(nms[:], negm[:], SHIFT, None, ALU.add), b, "parts", 1)
                step(dve.tensor_copy(nmp[:, :, 0, :], nms[:]), b, "parts", 2)
                step(dve.tensor_tensor(nmr1[:], nms[:], nmp[:, :, 0, :], ALU.subtract), b, "parts", 3)
                step(dve.tensor_copy(nmp[:, :, 1, :], nmr1[:]), b, "parts", 4)
                dve.tensor_tensor(nmp[:, :, 2, :], nmr1[:], nmp[:, :, 1, :], ALU.subtract).then_inc(nmp_ready, 1)

            def residual(b, k):
                g, kk, _, _ = tile_of(k)
                dve.wait_ge(t_done, val(b, lambda t: NK * t + k + 1))
                if kk < 2:
                    wait(dve, o_full, val(b, lambda t: 2 * NJ * (t - 1) + NJ * (g + 1) if t else 0))
                dve.tensor_tensor(pb[g][:, kk, :], p32[:, k % 2, :], pa[g][:, kk, :], ALU.subtract
                                  ).then_inc(pb_dve, 1)

            def sum_o(b, g, j):
                dve.wait_ge(o_full, val(b, lambda t: 2 * NJ * t + NJ * g + j + 1))
                wait(dve, on_ready, val(b, lambda t: max(0, 2 * NJ * t + NJ * g + j - 1)))
                o = ps_o[j % 2][:, 0:HG * VW].rearrange("p (h e) -> p h e", e=VW)
                dve.tensor_reduce(osum[:, j % 2], o[:, :, 0:3 * HD].rearrange("p h (x d) -> p h d x", x=3),
                                  X, ALU.add)
                dve.reciprocal(rden[:, j % 2], o[:, :, 3 * HD]).then_inc(o_free, 1)

            def add_x(b, p):
                dve.wait_ge(late_consts_in, 80)
                dve.wait_ge(xres_in[b.par], val(b, lambda t: 16 * (t // 2 + 1)))
                src = full(dve, b, f"wo{p}")
                if p == 0:
                    wait(dve, z_ready, val(b, lambda t: t))
                dve.tensor_tensor(x1[:, 2 * p:2 * p + 2, :], xres[b.par][:, 2 * p:2 * p + 2, :],
                                  src[:].rearrange("p (j d) -> p j d", j=2), ALU.add).then_inc(x1_ready, 1)
                dve.wait_ge(x1_ready, val(b, lambda t: 2 * t + p + 1))
                dve.sem_inc(d_free[p], 1)

            def gate_a(b):
                src = full(dve, b, "logit")
                g = "gate_a"
                step(dve.tensor_copy(g_l[:], src[0:1, 0:E]), b, g, 1)
                dve.sem_inc(d_free[0], 1)
                l_j = g_l[:].unsqueeze(1).broadcast_to([1, E, E])
                l_e = g_l[:].unsqueeze(2).broadcast_to([1, E, E])
                mark(dve.tensor_tensor(g_eq[:], l_j, l_e, ALU.is_equal))
                mark(dve.tensor_tensor(g_gt[:], l_j, l_e, ALU.is_gt))
                step(dve.tensor_reduce(g_s[:, 0:1], g_l[:], X, ALU.max), b, g, 4)
                step(dve.tensor_tensor(g_eq[:], g_eq[:], tri_sb[:].rearrange("a (e j) -> a e j", j=E), ALU.mult),
                     b, g, 5)
                step(dve.tensor_tensor(g_gt[:], g_gt[:], g_eq[:], ALU.add), b, g, 6)
                step(dve.tensor_reduce(g_sel[:, 3, :], g_gt[:], X, ALU.add), b, g, 7)
                step(dve.tensor_single_scalar(g_sel[:, 0, :], g_sel[:, 3, :], 2.0, ALU.is_lt), b, g, 8)
                dve.tensor_scalar(g_sel[:, 1, :], g_l[:], g_s[:, 0:1], None, ALU.subtract).then_inc(g_diff, 1)

            def gate_b(b):
                g = "gate_b"
                dve.wait_ge(g_exp, val(b, lambda t: t // 2 + 1))
                step(dve.tensor_tensor(g_sel[:, 4, :], g_sel[:, 2, :], g_sel[:, 0, :], ALU.mult), b, g, 1)
                step(dve.tensor_reduce(g_s[:, 1:2], g_sel[:, 4, :], X, ALU.add), b, g, 2)
                step(dve.reciprocal(g_s[:, 2:3], g_s[:, 1:2]), b, g, 3)
                dve.tensor_scalar(g_row[:], g_sel[:, 4, :].unsqueeze(2).broadcast_to([1, E, R]), g_s[:, 2:3], None,
                                  ALU.mult).then_inc(g_row_ready, 1)

            def gate_col(b):
                src = full(dve, b, "gcol")
                wait(dve, d_free[0], val(b, lambda t: ordinal["down", t - 1] if t else 0))
                dve.tensor_copy(g_col[:], src[:, 0:1]).then_inc(g_col_ready, 1)
                dve.wait_ge(g_col_ready, val(b, lambda t: t // 2 + 1))
                dve.sem_inc(d_free[1], 1)

            def add_z(b, p):
                name = f"up{p}"
                src = full(dve, b, name)
                dve.wait_ge(z_ready, val(b, lambda t: t + 1))
                if p == 0:
                    wait(dve, y_out, val(b, lambda t: 16 * t))
                dve.tensor_tensor(y[:, 2 * p:2 * p + 2, :], z[:, 2 * p:2 * p + 2, :],
                                  src[:].rearrange("p (j d) -> p j d", j=2), ALU.add).then_inc(y_ready, 1)
                dve.wait_ge(y_ready, val(b, lambda t: 2 * t + p + 1))
                dve.sem_inc(d_free[bank_of[name]], 1)

            b0 = Blk(0, 0)
            dve.memset(v_n[:], 0.0).then_inc(v_zero, 1)
            dve.wait_ge(v_zero, 1)
            dve.memset(v_n[:, :, 0:HG * VW].rearrange("p g (h e) -> p g h e", e=VW)[:, :, :, VW - 1], 1.0
                       ).then_inc(dve_cleared, 1)
            for q in range(4):
                v = v_n[32 * q:32 * q + TAIL].rearrange("p g (a gg h e) -> p g a gg h e", a=2, gg=2, e=VW)
                ins = dve.memset(v[:, :, 1, :, q, VW - 1], 1.0)
            ins.then_inc(dve_cleared, 1)
            dve.memset(kst_n[NROW:NMAX], 1.0).then_inc(dve_cleared, 1)
            dve.memset(one1[:], 1.0).then_inc(one_ready, 1)
            ln1(b0)
            dve.wait_ge(consts_in, 64)
            dve.tensor_copy(id16[:], id32[:]).then_inc(id16_ready, 1)
            k_rest(b0)
            k3(b0)
            v_rest(b0)
            v3(b0)
            q_rest(b0)
            q3(b0)
            ln1(b0.at(1))
            dve.wait_ge(masks_in, 96)
            for dst, src in ((maskq, m8), (maskk, mt8), (maskt, mtt8)):
                dve.tensor_scalar(dst[:], src[:], -MASKED, MASKED, ALU.mult, ALU.add).then_inc(masks_ready, 1)
            q_rest(b0.at(1))
            q3(b0.at(1))
            for u in range(len(UNITS)):
                maxima(b0, u)
            max_parts(b0)

            def slot(sl):
                for k in range(NK):
                    if k == 2 and sl.has_project:
                        ln1(sl.prj)
                    if sl.has_maxima:
                        for kb, j in units_at(k):
                            maxima(sl.nxt, kb * NJ + j)
                    if k not in POOL_TILES:
                        residual(sl.b, k)
                    if k == 1 and sl.has_kv:
                        k_rest(sl.b.at(2))
                    if k == 2 and sl.has_kv:
                        k3(sl.b.at(2))
                        v_rest(sl.b.at(2))
                    if k == 3 and sl.has_kv:
                        v3(sl.b.at(2))
                    if k == 5 and sl.has_finish:
                        add_x(sl.fin, 0)
                        add_x(sl.fin, 1)
                        ln2(sl.fin)
                    if k == 7 and sl.has_project:
                        q_rest(sl.prj)
                    if k == 8 and sl.has_project:
                        q3(sl.prj)
                    if k == 10 and sl.has_finish and sl.fin.par == 0:
                        gate_a(sl.fin)
                    if k == 11 and sl.has_finish and sl.fin.par == 0:
                        gate_b(sl.fin)
                    if k == 12 and sl.has_finish and sl.fin.par == 0:
                        gate_col(sl.fin)
                    if 12 <= k < 16:
                        sum_o(sl.b, 0, k - 12)
                    if k == 15 and sl.has_finish:
                        add_z(sl.fin, 0)
                        add_z(sl.fin, 1)
                if sl.has_maxima:
                    max_parts(sl.nxt)
                for j in range(NJ):
                    sum_o(sl.b, 1, j)

            run(dve, slot)
            last = Blk(NB, -1)
            add_x(last, 0)
            add_x(last, 1)
            ln2(last)
            add_z(last, 0)
            add_z(last, 1)

        @block.tensor
        def _(pe):
            def project_kv(b, v):
                if not v:
                    pe.wait_ge(ctx_in, val(b, lambda t: 16 * (t // 2 + 1)))
                    for m in range(2):
                        dst = fill(pe, b, f"k{m}")
                        for c in range(KC):
                            mm = pe.matmul(dst[:, 0:SK], wk[:, c, P * m:P * m + P], cin[:, c, :],
                                           start=c == 0, stop=c == KC - 1)
                        mm.then_inc(d_full[m], 1)
                    return
                dst = fill(pe, b, "v0")
                for c in range(KC):
                    mm = pe.matmul(dst[:, 0:D], cin[:, c, 0:P], wv[:, c, :], start=c == 0, stop=c == KC - 1)
                mm.then_inc(d_full[0], 1)
                pe.wait_ge(tail_copied, val(b, lambda t: t // 2 + 1))
                dst = fill(pe, b, "v1")
                for c in range(KC):
                    mm = pe.matmul(dst[:, 0:D], ctail[:, c].rearrange("p q k -> p (q k)"), wv[:, c, :],
                                   start=c == 0, stop=c == KC - 1)
                mm.then_inc(d_full[1], 1)

            def turn(b, names, src):
                for c, name in enumerate(names):
                    dst = fill(pe, b, name)
                    for j in range(NJ):
                        mm = pe.transpose(dst[:, P * j:P * j + P], src[:, j, P * c:P * c + P], id32[:])
                    mm.then_inc(d_full[c], 1)

            def project_q(b):
                for c in range(KC):
                    pe.wait_ge(d_free[c], nth(b, f"xT{c}"))
                for m in range(2):
                    dst = fill(pe, b, f"q{m}")
                    for c in range(KC):
                        mm = pe.matmul(dst[:], wq[:, c, P * m:P * m + P], xnT[:, c, :], start=c == 0,
                                       stop=c == KC - 1)
                    mm.then_inc(d_full[m], 1)

            def score_unit(b, u):
                kb, j = UNITS[u]
                h0 = HPB * kb
                n = min(HPB, H - h0)
                if u == 0:
                    pe.wait_ge(kst_n_in, val(b, lambda t: 16 * 6 * (t // 2 + 1)))
                    pe.wait_ge(q_stack[b.par][0], val(b, lambda t: 48 * (t // 2 + 1)))
                if kb == 2 and j == 0:
                    pe.wait_ge(q_stack[b.par][1], val(b, lambda t: 48 * (t // 2 + 1)))
                wait(pe, s_free, val(b, lambda t: max(0, len(UNITS) * t + u - 1)))
                dst = ps_s[u % 2]
                pe.matmul(dst[:, 0:n * SK].rearrange("p (h k) -> p h k", k=SK), id16[:],
                          maskq[:, NJ * b.par + j, :].unsqueeze(1).broadcast_to([P, n, SK]),
                          start=True, stop=False, skip_group_check=True)
                for h in range(n):
                    mm = pe.matmul(dst[:, h * SK:(h + 1) * SK], qst[b.par][0:NROW, h0 + h, P * j:P * j + P],
                                   kst_n[0:NROW, h0 + h, 0:SK], start=False, stop=h == n - 1,
                                   skip_group_check=True)
                mm.then_inc(s_full, 1)

            def score_tile(b, k):
                g, kk, gg, hq = tile_of(k)
                if k == 0:
                    pe.wait_ge(nm_rows[b.par], val(b, lambda t: 48 * (t // 2 + 1)))
                if kk == 0:
                    pe.wait_ge(kst_c_in[g], val(b, lambda t: 16 * (t // 2 + 1)))
                wait(pe, t_done, val(b, lambda t: max(0, NK * t + k - 1)))
                dst = ps_t[k % 2]
                h0 = HG * g + 4 * gg
                cols = slice(QB * b.par, QB * b.par + QB)
                if hq < 4:
                    pe.matmul(dst[:], kst_c[:, h0 + hq, 0:P], qst[b.par][:, h0 + hq, :], start=True, stop=False)
                    pe.matmul(dst[:], id16[:], maskk[:, cols], start=False, stop=True).then_inc(t_full, 1)
                    return
                for q in range(4):
                    pe.matmul(dst[32 * q:32 * q + 32, :], kst_c[:, h0 + q, P:SKP], qst[b.par][:, h0 + q, :],
                              start=True, stop=False, skip_group_check=True)
                pe.matmul(dst[:], id16[:], maskt[:, cols], start=False, stop=True,
                          skip_group_check=True).then_inc(t_full, 1)

            def pv(b, g, j):
                if j == 0:
                    pe.wait_ge(pb_dve, val(b, lambda t: pb_count(NK * t + NT * (g + 1), False)))
                    pe.wait_ge(pb_pool, val(b, lambda t: pb_count(NK * t + NT * (g + 1), True)))
                    pe.wait_ge(v_c_in[g], val(b, lambda t: 16 * (t // 2 + 1)))
                wait(pe, o_free, val(b, lambda t: max(0, 2 * NJ * t + NJ * g + j - 1)))
                dst = ps_o[j % 2]
                first = True
                for half, part in enumerate((pa[g], pb[g])):
                    for kk in range(NT):
                        gg, hq = divmod(kk, 5)
                        if hq < 4:
                            at, w, v = (4 * gg + hq) * VW, VW, (4 * gg + hq) * VW
                        else:
                            at, w, v = 4 * gg * VW, 4 * VW, (HG + 4 * gg) * VW
                        mm = pe.matmul(dst[:, at:at + w], part[:, kk, P * j:P * j + P], v_c[:, g, v:v + w],
                                       start=first, stop=half == 1 and kk == NT - 1, skip_group_check=True)
                        first = False
                mm.then_inc(o_full, 1)

            def apply_wo(b):
                for c in range(KC):
                    pe.wait_ge(d_free[c], nth(b, f"oT{c}"))
                pe.wait_ge(late_consts_in, 80)
                for p in range(2):
                    dst = fill(pe, b, f"wo{p}")
                    for j in range(2):
                        for c in range(KC):
                            mm = pe.matmul(dst[:, D * j:D * j + D], oT[:, c, P * (2 * p + j):P * (2 * p + j) + P],
                                           wo[:, c, :], start=c == 0, stop=c == KC - 1, skip_group_check=True)
                    mm.then_inc(d_full[p], 1)

            def x2_turn(b):
                pe.wait_ge(x2_ready, val(b, lambda t: NJ * (t + 1)))
                turn(b, ("x2T0", "x2T1"), x2)

            def logits(b):
                for c in range(KC):
                    pe.wait_ge(d_free[c], nth(b, f"x2T{c}"))
                dst = fill(pe, b, "logit")
                for c in range(KC):
                    mm = pe.matmul(dst[0:1, 0:E], x2T[:, c, 0:1], wrout[:, c, :], start=c == 0, stop=c == KC - 1)
                mm.then_inc(d_full[0], 1)

            def gate_col(b):
                pe.wait_ge(one_ready, 1)
                pe.wait_ge(g_row_ready, val(b, lambda t: t // 2 + 1))
                dst = fill(pe, b, "gcol")
                pe.matmul(dst[:, 0:1], g_row[:].rearrange("a e r -> a (e r)"), one1[:], start=True, stop=True
                          ).then_inc(d_full[1], 1)

            def down(b):
                for c in range(KC):
                    pe.wait_ge(d_free[c], nth(b, f"x2T{c}"))
                dst = fill(pe, b, "down")
                for c in range(KC):
                    mm = pe.matmul(dst[:], wdown[:, c, :], x2T[:, c, :], start=c == 0, stop=c == KC - 1)
                mm.then_inc(d_full[0], 1)

            def up(b):
                pe.wait_ge(d_free[0], nth(b, "down"))
                for p in range(2):
                    name = f"up{p}"
                    dst = fill(pe, b, name)
                    for j in range(2):
                        mm = pe.matmul(dst[:, D * j:D * j + D], dn[:, P * (2 * p + j):P * (2 * p + j) + P], wup[:],
                                       start=True, stop=True, skip_group_check=True)
                    mm.then_inc(d_full[bank_of[name]], 1)

            def project(b):
                pe.wait_ge(xn_ready, val(b, lambda t: NJ * (t + 1)))
                turn(b, ("xT0", "xT1"), xn)

            def max_turn(b):
                dst = fill(pe, b, "nmT")
                hold(pe, nmp_ready, val(b, lambda t: t + 1))
                for j in range(NJ):
                    mm = pe.transpose(dst[0:3 * H, 64 * j:64 * j + 64].bitcast(BF16),
                                      nmp[:, j].rearrange("p a h -> p (a h)"), id16[:])
                mm.then_inc(d_full[1], 1)

            b0 = Blk(0, 0)
            pe.wait_ge(consts_in, 64)
            project_kv(b0, False)
            project_kv(b0, True)
            project(b0)
            project_q(b0)
            project(b0.at(1))
            project_q(b0.at(1))
            pe.wait_ge(id16_ready, 1)
            pe.wait_ge(masks_ready, 3)
            for u in range(len(UNITS)):
                score_unit(b0, u)
            max_turn(b0)

            def slot(sl):
                for k in range(NK):
                    score_tile(sl.b, k)
                    if sl.has_kv and k in (1, 2):
                        project_kv(sl.b.at(2), k == 2)
                    if sl.has_finish and k == 3:
                        pe.wait_ge(on_ready, val(sl.fin, lambda t: 2 * NJ * (t + 1)))
                        turn(sl.fin, ("oT0", "oT1"), on)
                    if sl.has_finish and k == 5:
                        apply_wo(sl.fin)
                    if sl.has_project and k == 6:
                        project(sl.prj)
                    if sl.has_project and k == 7:
                        project_q(sl.prj)
                    if sl.has_maxima:
                        for kb, j in units_at(k):
                            score_unit(sl.nxt, kb * NJ + j)
                    if sl.has_finish:
                        if k == 9:
                            x2_turn(sl.fin)
                        if k == 10 and sl.fin.par == 0:
                            logits(sl.fin)
                        if k == 12:
                            if sl.fin.par == 0:
                                gate_col(sl.fin)
                            down(sl.fin)
                        if k == 14:
                            up(sl.fin)
                    if 12 <= k < 16:
                        pv(sl.b, 0, k - 12)
                if sl.has_maxima:
                    max_turn(sl.nxt)
                for j in range(NJ):
                    pv(sl.b, 1, j)

            run(pe, slot)
            last = Blk(NB, -1)
            pe.wait_ge(on_ready, 2 * NJ * NBLK)
            turn(last, ("oT0", "oT1"), on)
            apply_wo(last)
            x2_turn(last)
            down(last)
            up(last)


def kernel(x, ctx_1024, mask_1x1xSxS2_bk0, L0_xattn_W_q, L0_xattn_W_k, L0_xattn_W_v, L0_xattn_W_o,
           L0_ffn_router_w, L0_ffn_lora_down, L0_ffn_lora_up):
    import numpy as np
    import concourse.bacc as bacc
    from concourse.bass_utils import run_bass_kernel_spmd

    def laid(a):
        return np.ascontiguousarray(a)

    def by_pairs(w):
        return laid(np.asarray(w).T.reshape(D, H // 2, 2, HD).transpose(0, 2, 1, 3).reshape(D, D))

    mask2 = np.asarray(mask_1x1xSxS2_bk0).reshape(S, SK)
    arrays = {
        "x": laid(np.asarray(x).reshape(NB * S, D)),
        "ctxT": laid(np.asarray(ctx_1024).transpose(0, 2, 1)),
        "mask": laid(mask2),
        "maskT": laid(mask2.T),
        "wqT": by_pairs(L0_xattn_W_q),
        "wkT": by_pairs(L0_xattn_W_k),
        "wvT": laid(np.asarray(L0_xattn_W_v).T),
        "woT": laid(np.asarray(L0_xattn_W_o).T),
        "routerT": laid(np.asarray(L0_ffn_router_w).T),
        "downT": laid(np.asarray(L0_ffn_lora_down).reshape(E * R, D).T),
        "upT": laid(np.asarray(L0_ffn_lora_up).transpose(0, 2, 1).reshape(E * R, D)),
        "ident": np.eye(P, dtype=np.float32),
        "tri": np.tril(np.ones((E, E), np.float32), -1).reshape(1, E * E),
    }
    nc = bacc.Bacc("TRN2", target_bir_lowering=False, num_devices=1)
    args = [nc.dram_tensor(n, a.shape, mybir.dt.from_np(a.dtype), kind="ExternalInput").ap()
            for n, a in arrays.items()]
    out = nc.dram_tensor("out", (NB * S, D), F32, kind="ExternalOutput").ap()
    build(nc, *args, out)
    r = run_bass_kernel_spmd(nc, [arrays], core_ids=[0])
    return r.results[0]["out"].reshape(NB, S, D)
```

```python
from contextlib import ExitStack

import concourse.bass as bass
from concourse import mybir

F32 = mybir.dt.float32
BF16 = mybir.dt.bfloat16
F16 = mybir.dt.float16
U8 = mybir.dt.uint8
I32 = mybir.dt.int32
ALU = mybir.AluOpType
ACT = mybir.ActivationFunctionType
X = mybir.AxisListType.X

D, H, HD = 256, 16, 16
NB, S, SK = 4, 1024, 154
E, R = 8, 16
P = 128
QB = 512
NJ = QB // P
NBLK = NB * S // QB
KC = D // P
TAIL = SK - P
SKP = P + 32
SLOTQ = (0, 0, 0, 1, 1, 2)
SLOTK = (0, 1, 2, 0, 1, 0)
NROW = 16 * len(SLOTQ)
NMAX = NROW + 3
VW = 3 * HD + 1
HG = H // 2
VG = 2 * HG * VW
NT = 10
NK = 2 * NT
HPB = 3
NU = (H + HPB - 1) // HPB
MASKED = -float(2 ** 99)
SHIFT = 9.704060527839234
EPS = 1e-5
NRING = 4
RSQRT_BITS = float(0x5F3759DF)
NEWTON = 3
SCALE = 0.25


PE_AT = {
    "tile": tuple(range(NK)),
    "pv1": (0.02, 0.35, 0.54, 2.66),
    "pv0": (15.67, 15.9, 17.9, 18.9),
    "unit": (0.3, 1.3, 2.38, 3.3, 4.46, 5.3, 6.14, 7.32, 7.46, 8.14, 9.14, 9.32, 10.02, 10.94, 11.4, 12.3, 13.3,
        13.4, 14.22, 15.22, 15.68, 16.5, 17.88, 17.95),
    "k": (2.46, 3.49),
    "v": (5.39, 5.49),
    "oT": (5.59, 5.8),
    "wo": (7.08, 7.5),
    "xT": (9.5, 9.8),
    "max": (10.1, 19.95),
    "q": (11.39, 11.4),
    "nT": (12.48, 13.01),
    "logit": 15.41,
    "gcol": 17.83,
    "down": 16.31,
    "up": (18.62, 18.83),
}
ACT_AT = {
    "exp": tuple(range(NK)),
    "k1": (2.78, 3.08),
    "k2": (3.14, 3.56),
    "v1": (4.64, 4.74),
    "v2": (5.3, 5.31),
    "oT": (5.59, 5.69),
    "norm1_x": (8.68, 8.79, 8.89, 8.92),
    "xT": (9.31, 10.04),
    "norm2_x": (10.36, 10.37, 10.5, 10.8),
    "max": (10.2, 19.22),
    "q1": (10.99, 11.01),
    "q2": (12.47, 12.84),
    "nT": (13.19, 13.31),
    "gexp": 14.74,
    "down": 17.5,
    "store": 18.42,
}
DVE_AT = {
    "pb": {1: 1.51, 10: 10.92, 18: 18.4, 19: 19.4},
    "sum1": (0.25, 0.25, 1.7, 2.78),
    "sum0": (16.02, 16.73, 18.02, 19.95),
    "unit": (0.3, 1.3, 2.38, 3.46, 4.46, 5.46, 6.14, 7.3, 7.43, 8.14, 9.14, 9.27, 10.02, 10.94, 11.35, 11.6,
        12.6, 12.65, 14.22, 15.22, 15.63, 16.5, 17.88, 17.9),
    "kr": (3.16, 3.26),
    "k3": (3.6, 4.53),
    "vr": (4.7, 5.03),
    "v3": (6.16, 6.26),
    "ln1a": (0.33, 1, 1.2, 2.19),
    "ln1b": 3.57,
    "addx": (7.5, 7.85),
    "ln2a": (7.7, 7.8, 9.25, 9.35),
    "ln2b": 9.36,
    "max": (9.46, 18.27),
    "qr": (11.11, 11.72),
    "q3": (12.6, 13.11),
    "gate_a": 14.91,
    "gate_b": 15.92,
    "gcol": 16.27,
    "y": (18.15, 18.16),
}
POOL_AT = {
    "pb": {0: 0.02, 2: 2.01, 3: 3.01, 4: 4.01, 5: 5.01, 6: 6.49, 7: 7.01, 8: 8.01, 9: 9.01, 11: 11.01, 12:
        12.01, 13: 13.01, 14: 14.01, 15: 15.01, 16: 16.01, 17: 17.4},
    "o_norm1": (0.25, 1.25, 1.25, 1.32),
    "o_norm0": (14.6, 18.1, 18.95, 18.95),
    "tail": 0.99,
    "scales1": 4.93,
    "scales2": 8.46,
    "z": 9.04,
}
PE_FIRST = (
    ("k", 0), ("xT", 0), ("q", 0), ("v", 0), ("unit", 0, range(0, 6)), ("xT", 1), ("unit", 0, range(6, 12)),
    ("q", 1), ("unit", 0, range(12, 18)), ("unit", 0, range(18, 24)), ("max", 0, range(0, 1)), ("max", 0,
    range(1, 2)),
)
ACT_FIRST = (
    ("k1", 0), ("norm1_x", 0), ("k2", 0), ("xT", 0), ("q1", 0), ("v1", 0), ("q2", 0), ("v2", 0), ("norm1_x", 1),
    ("xT", 1), ("q1", 1), ("q2", 1), ("max", 0, range(0, 1)), ("max", 0, range(1, 2)),
)
DVE_FIRST = (
    ("ln1a", 0), ("ln1b", 0), ("id16", 0), ("kr", 0), ("k3", 0), ("ln1a", 1), ("qr", 0), ("masks", 0), ("vr",
    0), ("q3", 0), ("v3", 0), ("ln1b", 1), ("unit", 0, range(0, 6)), ("unit", 0, range(6, 12)), ("qr", 1),
    ("unit", 0, range(12, 18)), ("q3", 1), ("max", 0, range(0, 1)), ("unit", 0, range(18, 24)), ("max", 0,
    range(1, 2)),
)
KV_STAGES = ("k", "v", "k1", "k2", "v1", "v2", "kr", "k3", "vr", "v3", "tail")
PROJECT_STAGES = ("xT", "q", "norm1_x", "q1", "q2", "ln1a", "ln1b", "qr", "q3", "scales1")
MAXIMA_STAGES = ("unit", "max")
ATTEND_STAGES = ("tile", "exp", "pb", "pv0", "sum0", "o_norm0")
GATE_STAGES = ("logit", "gcol", "gexp", "gate_a", "gate_b")


class Blk:

    def __init__(self, i, o):
        self.i, self.o, self.par = i, o, o % 2

    def at(self, d):
        return Blk(self.i, self.o + d)

    def row(self):
        return self.i * (2 * QB) + self.o * QB


def build(nc, x, ctxT, mask, maskT, wqT, wkT, wvT, woT, routerT, downT, upT, ident, tri, out):
    with ExitStack() as es:
        def sb(name, shape, dt=F32):
            return es.enter_context(nc.sbuf_tensor(name, shape, dt))

        def psum(name):
            return es.enter_context(nc.psum_tensor(name, [P, 512], F32))

        def sem(name):
            return es.enter_context(nc.semaphore(name))

        wq, wk, wv, wo = (sb(n, [P, KC, D]) for n in ("wq", "wk", "wv", "wo"))
        wdown = sb("wdown", [P, KC, E * R])
        wup = sb("wup", [P, D])
        wrout = sb("wrout", [P, KC, E])
        id32 = sb("id32", [P, P])
        id16 = sb("id16", [P, P], BF16)
        tri_sb = sb("tri_sb", [1, E * E])
        one1 = sb("one1", [1, 1])
        m8 = sb("m8", [P, S // P, SK], U8)
        mt8 = sb("mt8", [P, S], U8)
        mtt8 = sb("mtt8", [P, S], U8)
        maskq = sb("maskq", [P, S // P, SK], BF16)
        maskk = sb("maskk", [P, S], BF16)
        maskt = sb("maskt", [P, S], BF16)
        cin = sb("cin", [P, KC, SK])
        ctail = sb("ctail", [P, KC, 4, 32])
        kp = sb("kp", [P, 3, 2, SKP], BF16)
        kr = sb("kr", [P, 2, SK])
        kst_n = sb("kst_n", [NMAX, H, SKP], BF16)
        kst_c = sb("kst_c", [NMAX, H, SKP], BF16)
        v_n = sb("v_n", [P, 2, VG], BF16)
        v_c = sb("v_c", [P, 2, VG], BF16)
        vr = sb("vr", [P, 2, D])
        kdram = nc.dram_tensor("kdram", [3, HD, H, SKP], BF16).ap()
        qdram = nc.dram_tensor("qdram", [3, HD, H, QB], BF16).ap()
        xin = [sb(f"xin{s}", [P, NJ, D]) for s in range(2)]
        xres = [sb(f"xres{s}", [P, NJ, D]) for s in range(2)]
        stats = sb("stats", [P, NJ, 6])
        mv = sb("mv", [P, NJ, 2])
        rstd = sb("rstd", [P, NJ])
        nmr = sb("nmr", [P, NJ])
        stats2 = sb("stats2", [P, NJ, 6])
        mv2 = sb("mv2", [P, NJ, 2])
        rstd2 = sb("rstd2", [P, NJ])
        nmr2 = sb("nmr2", [P, NJ])
        var = sb("var", [P, NJ])
        var2 = sb("var2", [P, NJ])
        newt = sb("newt", [P, NJ])
        xn = sb("xn", [P, NJ, D])
        xnT = sb("xnT", [P, KC, QB])
        qp = sb("qp", [P, 3, 2, QB], BF16)
        qr = sb("qr", [P, 2, QB])
        qst = [sb(f"qst{s}", [NMAX, H, QB], BF16) for s in range(2)]
        negm = sb("negm", [P, NJ, H])
        nms = sb("nms", [P, NJ, HG])
        nmp = [sb(f"nmp{g}", [P, NJ, 3, HG], BF16) for g in range(2)]
        nmr1 = sb("nmr1", [P, NJ, HG])
        nmT = [sb(f"nmT{g}", [3 * HG, QB], BF16) for g in range(2)]
        p32 = sb("p32", [P, NRING, QB])
        pa = [sb(f"pa{g}", [P, NT, QB], F16) for g in range(2)]
        pb = [sb(f"pb{g}", [P, NT, QB], F16) for g in range(2)]
        osum = sb("osum", [P, 2, HG, HD])
        rden = sb("rden", [P, 2, HG])
        on = sb("on", [P, NJ, D])
        oT = sb("oT", [P, KC, QB])
        x1 = sb("x1", [P, NJ, D])
        x2 = sb("x2", [P, NJ, D])
        z = sb("z", [P, NJ, D])
        x2T = sb("x2T", [P, KC, QB])
        dn = sb("dn", [P, QB])
        y = sb("y", [P, NJ, D])
        g_l = sb("g_l", [1, E])
        g_eq = sb("g_eq", [1, E, E])
        g_gt = sb("g_gt", [1, E, E])
        g_sel = sb("g_sel", [1, 8, E])
        g_s = sb("g_s", [1, 4])
        g_row = sb("g_row", [1, E, R])
        g_col = sb("g_col", [P, 1])

        ps_s = [psum(f"ps_s{k}") for k in range(2)]
        ps_t = [psum(f"ps_t{k}") for k in range(2)]
        ps_o = [psum(f"ps_o{k}") for k in range(2)]
        ps_d = [psum(f"ps_d{k}") for k in range(2)]

        passed = sem("passed")
        consts_in = sem("consts_in")
        late_consts_in = sem("late_consts_in")
        masks_in = sem("masks_in")
        pool_cleared = sem("pool_cleared")
        dve_cleared = sem("dve_cleared")
        id16_ready = sem("id16_ready")
        masks_ready = sem("masks_ready")
        ctx_in = sem("ctx_in")
        tail_copied = sem("tail_copied")
        x_in = [sem(f"x_in{s}") for s in range(2)]
        xres_in = [sem(f"xres_in{s}") for s in range(2)]
        dve_step = sem("dve_step")
        act_step = sem("act_step")
        pool_step = sem("pool_step")
        d_full = [sem(f"d_full{k}") for k in range(2)]
        d_free = [sem(f"d_free{k}") for k in range(2)]
        ln1_stats = sem("ln1_stats")
        ln1_scale = sem("ln1_scale")
        ln2_scale = sem("ln2_scale")
        xn_ready = sem("xn_ready")
        q1_ready = sem("q1_ready")
        qr_ready = sem("qr_ready")
        q2_ready = sem("q2_ready")
        q3_ready = sem("q3_ready")
        q_dram = sem("q_dram")
        q_stack = [[sem(f"q_stack{s}{g}") for g in range(2)] for s in range(2)]
        v_zero = sem("v_zero")
        k1_ready = sem("k1_ready")
        kr_ready = sem("kr_ready")
        k2_ready = sem("k2_ready")
        k3_ready = sem("k3_ready")
        k_dram = sem("k_dram")
        kst_n_in = sem("kst_n_in")
        kst_c_in = [sem(f"kst_c_in{g}") for g in range(2)]
        v1_ready = sem("v1_ready")
        vr_ready = sem("vr_ready")
        v2_ready = sem("v2_ready")
        v3_ready = sem("v3_ready")
        v_c_in = [sem(f"v_c_in{g}") for g in range(2)]
        s_full = sem("s_full")
        s_free = sem("s_free")
        nmp_ready = [sem(f"nmp_ready{g}") for g in range(2)]
        nm_rows = [[sem(f"nm_rows{s}{g}") for g in range(2)] for s in range(2)]
        t_full = sem("t_full")
        t_done = sem("t_done")
        pb_dve = sem("pb_dve")
        pb_pool = sem("pb_pool")
        o_full = sem("o_full")
        o_free = sem("o_free")
        on_ready = sem("on_ready")
        x1_ready = sem("x1_ready")
        ln2_stats = sem("ln2_stats")
        x2_ready = sem("x2_ready")
        z_ready = sem("z_ready")
        g_diff = sem("g_diff")
        g_exp = sem("g_exp")
        g_row_ready = sem("g_row_ready")
        one_ready = sem("one_ready")
        g_col_ready = sem("g_col_ready")
        y_ready = sem("y_ready")
        y_out = sem("y_out")

        def val(b, f):
            if isinstance(b.i, int):
                return f(2 * b.i + b.o)
            at1, at2 = f(2 + b.o), f(4 + b.o)
            return b.i * (at2 - at1) + (2 * at1 - at2)

        def wait(eng, s, v):
            if not isinstance(v, int) or v > 0:
                eng.wait_ge(s, v)

        def hold(eng, s, v):
            wait(eng, s, v)
            eng.sem_inc(passed, 1)

        class Slot:
            def __init__(self, b, first, last):
                self.b = b
                self.has_finish = not (first and b.par == 0)
                self.has_project = not last
                self.has_maxima = not (last and b.par == 1)
                self.has_kv = not last and b.par == 0
                self.nxt, self.prj, self.fin = b.at(1), b.at(2), b.at(-1)

            def stages(self, table):
                at = []
                for name, pos in table.items():
                    if not isinstance(pos, dict):
                        pos = dict(enumerate(pos if isinstance(pos, tuple) else (pos,)))
                    at += [(p, name, part) for part, p in pos.items()]
                for _, name, part in sorted(at):
                    if name in ATTEND_STAGES:
                        yield name, self.b, part
                    elif name in KV_STAGES:
                        if self.has_kv:
                            yield name, self.prj, part
                    elif name in PROJECT_STAGES:
                        if self.has_project:
                            yield name, self.prj, part
                    elif name in MAXIMA_STAGES:
                        if self.has_maxima:
                            yield name, self.nxt, part
                    elif self.has_finish and (name not in GATE_STAGES or self.fin.par == 0):
                        yield name, self.fin, part

        def parts(table, name):
            return range(len(table[name]) if name in table and isinstance(table[name], tuple) else 1)

        def first_stages(order, table):
            for name, t, *some in order:
                for part in some[0] if some else parts(table, name):
                    yield name, Blk(0, t), part

        def slots():
            for b in range(NB):
                for par in range(2):
                    yield Slot(Blk(b, par), b == 0, b == NB - 1)

        BANKS = {"k": (0, 1), "v": (0, 1), "xT": (0, 1), "q": (0, 1), "oT": (0, 1), "wo": (0, 1),
                 "nT": (0, 1), "logit": (0,), "gcol": (1,), "down": (0,), "up": (1, 0), "max": (0, 1)}
        EPILOGUE = ("oT", "wo", "nT", "down", "up")
        uses = [(name, b.o, part) for name, b, part in first_stages(PE_FIRST, PE_AT) if name in BANKS]
        for sl in slots():
            uses += [(name, 2 * b.i + b.o, part) for name, b, part in sl.stages(PE_AT) if name in BANKS]
        uses += [(name, NBLK - 1, part) for name in EPILOGUE for part in range(len(BANKS[name]))]
        ordinal, bank_of, seen = {}, {}, [0, 0]
        for name, t, part in uses:
            bank = BANKS[name][part]
            seen[bank] += 1
            ordinal[f"{name}{part}", t] = seen[bank]
            bank_of[f"{name}{part}"] = bank

        def nth(b, name):
            return val(b, lambda t: ordinal[name, t])

        def fill(pe, b, name):
            k = bank_of[name]
            wait(pe, d_free[k], val(b, lambda t: ordinal[name, t] - 1))
            return ps_d[k]

        def full(eng, b, name):
            k = bank_of[name]
            eng.wait_ge(d_full[k], nth(b, name))
            return ps_d[k]

        def pb_count(n, on_pool):
            whole, rest = divmod(n, NK)
            mine = (POOL_AT if on_pool else DVE_AT)["pb"]
            return whole * len(mine) + sum(k < rest for k in mine)

        def tile_of(k):
            g, kk = divmod(k, NT)
            return g, kk, kk // 5, kk % 5

        def run(eng, slot):
            for s in range(2):
                slot(Slot(Blk(0, s), True, False))
            with eng.Fori(1, NB - 1) as i:
                for s in range(2):
                    slot(Slot(Blk(i, s), False, False))
            for s in range(2):
                slot(Slot(Blk(NB - 1, s), False, True))

        UNITS = [(kb, j) for kb in range(NU) for j in range(NJ)]

        block = es.enter_context(nc.Block())

        @block.sync
        def _(sp):
            def spread(part, src, dram, done):
                for_pairs = dram[part].rearrange("d (hh m) n -> hh d (m n)", m=2)
                sp.dma_start(for_pairs, src[:, part].rearrange("p m n -> p (m n)")).then_inc(done, 16)

            def q_to_dram(b):
                for g in range(2):
                    hold(sp, q_stack[(b.par + 1) % 2][g], val(b, lambda t: 48 * ((t - 1) // 2 + 1) if t else 0))
                for part, ready in enumerate((q1_ready, q2_ready, q3_ready)):
                    hold(sp, ready, val(b, lambda t: 2 * (t + 1)))
                    spread(part, qp, qdram, q_dram)

            def stack_q(b, g):
                hs = slice(HG * g, HG * g + HG)
                hold(sp, q_dram, val(b, lambda t: 48 * (t + 1)))
                hold(sp, t_full, val(b, lambda t: NK * (t - 2) + NT * (g + 1) if t >= 2 else 0))
                for part, to, n in ((0, 0, 3), (1, 3, 2), (2, 5, 1)):
                    sp.dma_start(qst[b.par][HD * to:HD * (to + n), hs, :],
                                 qdram[part, :, hs].unsqueeze(0).broadcast_to([n, HD, HG, QB])
                                 ).then_inc(q_stack[b.par][g], 16)

            def stack_k(b):
                for part, ready in enumerate((k1_ready, k2_ready, k3_ready)):
                    hold(sp, ready, val(b, lambda t: 2 * (t // 2 + 1)))
                    spread(part, kp, kdram, k_dram)
                hold(sp, s_full, val(b, lambda t: len(UNITS) * (t - 1) if t else 0))
                for g in range(2):
                    hold(sp, kst_c_in[g], val(b, lambda t: 16 * (t // 2)))
                hold(sp, k_dram, val(b, lambda t: 48 * (t // 2 + 1)))
                for to, n in ((0, 3), (3, 2), (5, 1)):
                    sp.dma_start(kst_n[HD * to:HD * (to + n)], kdram[0:n]).then_inc(kst_n_in, 16)

            def keys_to_attend(b, g):
                hold(sp, kst_n_in, val(b, lambda t: 48 * (t // 2 + 1)))
                hold(sp, t_full, val(b, lambda t: NK * (t - 1) + NT * (g + 1) if t else 0))
                sp.dma_start(kst_c[:, HG * g:HG * g + HG, :], kst_n[:, HG * g:HG * g + HG, :]
                             ).then_inc(kst_c_in[g], 16)
                hold(sp, v3_ready, val(b, lambda t: 5 * (t // 2 + 1)))
                hold(sp, o_full, val(b, lambda t: 2 * NJ * (t - 1) + NJ * (g + 1) if t else 0))
                sp.dma_start(v_c[:, g, :], v_n[:, g, :]).then_inc(v_c_in[g], 16)

            b0 = Blk(0, 0)
            sp.dma_start(wk[:], wkT.rearrange("(c p) n -> p c n", p=P)).then_inc(consts_in, 16)
            sp.dma_start(id32[:], ident).then_inc(consts_in, 16)
            sp.dma_start(wq[:], wqT.rearrange("(c p) n -> p c n", p=P)).then_inc(consts_in, 16)
            sp.dma_start(wv[:], wvT.rearrange("(c p) n -> p c n", p=P)).then_inc(consts_in, 16)
            sp.wait_ge(pool_cleared, 1)
            sp.dma_start(m8[:], mask.rearrange("(j p) k -> p j k", p=P)).then_inc(masks_in, 16)
            sp.dma_start(mt8[:], maskT[0:P, :]).then_inc(masks_in, 16)
            for q in range(4):
                sp.dma_start(mtt8[32 * q:32 * q + TAIL, :], maskT[P:SK, :]).then_inc(masks_in, 16)
            sp.wait_ge(dve_cleared, 3)
            stack_k(b0)
            q_to_dram(b0)
            for g in range(2):
                stack_q(b0, g)
            for g in range(2):
                keys_to_attend(b0, g)
            sp.dma_start(wo[:], woT.rearrange("(c p) n -> p c n", p=P)).then_inc(late_consts_in, 16)
            sp.dma_start(wdown[:], downT.rearrange("(c p) n -> p c n", p=P)).then_inc(late_consts_in, 16)
            sp.dma_start(wup[:], upT).then_inc(late_consts_in, 16)
            sp.dma_start(wrout[:], routerT.rearrange("(c p) n -> p c n", p=P)).then_inc(late_consts_in, 16)
            sp.dma_start(tri_sb[:], tri).then_inc(late_consts_in, 16)
            q_to_dram(b0.at(1))
            for g in range(2):
                stack_q(b0.at(1), g)

            def slot(sl):
                b = sl.b
                if sl.has_kv:
                    stack_k(b.at(2))
                if sl.has_project:
                    q_to_dram(sl.prj)
                    stack_q(sl.prj, 0)
                if b.par == 1 and sl.has_project:
                    keys_to_attend(b.at(1), 0)
                if sl.has_project:
                    stack_q(sl.prj, 1)
                if b.par == 1 and sl.has_project:
                    keys_to_attend(b.at(1), 1)

            run(sp, slot)
            sp.wait_ge(y_out, 16 * NBLK)

        @block.gpsimd
        def _(pool):
            order = [("ln1", 0), ("ln1", 1)]
            for sl in slots():
                order += [("ln" + name[-1], 2 * b.i + b.o) for name, b, _ in sl.stages(POOL_AT)
                          if name.startswith("scales")]
            order.append(("ln2", NBLK - 1))
            steps_of_norm = 4 * NEWTON + 1

            def scales(b, name, mv, var, rstd, nmr, stats_ready, ready):
                pool.wait_ge(stats_ready, val(b, lambda t: t + 1))
                n = 0
                for _ in range(NEWTON):
                    for what in range(4):
                        if what == 0:
                            ins = pool.tensor_tensor(newt[:], rstd[:], rstd[:], ALU.mult)
                        elif what == 1:
                            ins = pool.tensor_tensor(newt[:], newt[:], var[:], ALU.mult)
                        elif what == 2:
                            ins = pool.tensor_scalar(newt[:], newt[:], -0.5, 1.5, ALU.mult, ALU.add)
                        else:
                            ins = pool.tensor_tensor(rstd[:], rstd[:], newt[:], ALU.mult)
                        n += 1
                        ins.then_inc(pool_step, 1)
                        hold(pool, pool_step, val(b, lambda t: 1 + steps_of_norm * order.index((name, t)) + n))
                pool.tensor_tensor(nmr[:], mv[:, :, 0], rstd[:], ALU.mult).then_inc(pool_step, 1)
                hold(pool, pool_step, val(b, lambda t: 1 + steps_of_norm * order.index((name, t)) + n + 1))
                pool.tensor_scalar(nmr[:], nmr[:], -1.0, None, ALU.mult).then_inc(ready, 1)

            def scales1(b, part=0):
                scales(b, "ln1", mv, var, rstd, nmr, ln1_stats, ln1_scale)

            def scales2(b, part=0):
                scales(b, "ln2", mv2, var2, rstd2, nmr2, ln2_stats, ln2_scale)

            def copy_tail(b, part=0):
                pool.wait_ge(ctx_in, val(b, lambda t: 16 * (t // 2 + 1)))
                hold(pool, d_full[1], val(b, lambda t: ordinal["v1", t - 2] if t >= 2 else 0))
                for c in range(KC):
                    ins = pool.tensor_copy(ctail[:, c, :, 0:TAIL],
                                           cin[:, c, P:SK].unsqueeze(1).broadcast_to([P, 4, TAIL]))
                ins.then_inc(tail_copied, 1)

            def residual(b, k):
                g, kk, _, _ = tile_of(k)
                pool.wait_ge(t_done, val(b, lambda t: NK * t + k + 1))
                wait(pool, o_full, val(b, lambda t: 2 * NJ * (t - 1) + NJ * (g + 1) if t else 0))
                pool.tensor_tensor(pb[g][:, kk, :], p32[:, k % NRING, :], pa[g][:, kk, :],
                                   ALU.subtract).then_inc(pb_pool, 1)

            def normalise(b, g, j):
                pool.wait_ge(o_free, val(b, lambda t: 2 * NJ * t + NJ * g + j + 1))
                if g == 0 and j == 0:
                    wait(pool, d_full[1], val(b, lambda t: ordinal["oT1", t - 1] if t else 0))
                pool.tensor_tensor(on[:, j, P * g:P * g + P].rearrange("p (h d) -> p h d", d=HD),
                                   osum[:, j % 2], rden[:, j % 2].unsqueeze(2).broadcast_to([P, HG, HD]),
                                   ALU.mult).then_inc(on_ready, 1)

            def normalise0(b, j):
                normalise(b, 0, j)

            def normalise1(b, j):
                normalise(b, 1, j)

            def add_norms(b, part=0):
                pool.wait_ge(x2_ready, val(b, lambda t: NJ * (t + 1)))
                wait(pool, y_ready, val(b, lambda t: 2 * t))
                pool.tensor_tensor(z[:], x1[:], x2[:], ALU.add).then_inc(z_ready, 1)

            pool.memset(mtt8[:], 0).then_inc(pool_cleared, 1)
            pool.memset(kp[:], 0.0).then_inc(pool_cleared, 1)
            pool.memset(ctail[:], 0.0).then_inc(pool_step, 1)
            pool.wait_ge(pool_step, 1)
            scales1(Blk(0, 0))
            copy_tail(Blk(0, 0))
            scales1(Blk(0, 1))

            def slot(sl):
                do = {"pb": residual, "o_norm0": normalise0, "o_norm1": normalise1, "tail": copy_tail,
                      "scales1": scales1, "scales2": scales2, "z": add_norms}
                for name, b, part in sl.stages(POOL_AT):
                    do[name](b, part)

            run(pool, slot)
            for j in range(NJ):
                normalise(Blk(NB, -1), 1, j)
            scales2(Blk(NB, -1))
            add_norms(Blk(NB, -1))

        @block.scalar
        def _(act):
            def load_ctx(b):
                wait(act, d_full[1], val(b, lambda t: ordinal["v1", t - 2] if t >= 2 else 0))
                wait(act, tail_copied, val(b, lambda t: t // 2))
                bi = b.i + b.o // 2
                src = ctxT[bi:bi + 1] if isinstance(bi, int) else ctxT[bass.ds(bi, 1)]
                act.dma_start(cin[:], src.rearrange("a (c p) k -> p (a c) k", p=P)).then_inc(ctx_in, 16)

            def load_x(b):
                wait(act, xn_ready, val(b, lambda t: NJ * (t - 1)))
                act.dma_start(xin[b.par][:], x[bass.ds(b.row(), QB), :].rearrange("(j p) d -> p j d", p=P)
                             ).then_inc(x_in[b.par], 16)

            def load_xres(b):
                wait(act, x1_ready, val(b, lambda t: 2 * (t - 1)))
                act.dma_start(xres[b.par][:], x[bass.ds(b.row(), QB), :].rearrange("(j p) d -> p j d", p=P)
                             ).then_inc(xres_in[b.par], 16)

            def exps(b, k):
                g, kk, _, _ = tile_of(k)
                act.wait_ge(t_full, val(b, lambda t: NK * t + k + 1))
                engine_has = (k - NRING) % NK in POOL_AT["pb"]
                wait(act, pb_pool if engine_has else pb_dve,
                     val(b, lambda t: pb_count(NK * t + k - NRING + 1, engine_has) if NK * t + k >= NRING else 0))
                act.activation(p32[:, k % NRING, :], ps_t[k % 2][:], ACT.Exp)
                if kk == 0:
                    wait(act, o_full, val(b, lambda t: 2 * NJ * (t - 1) + NJ * (g + 1) if t else 0))
                act.activation(pa[g][:, kk, :], ps_t[k % 2][:], ACT.Exp).then_inc(t_done, 1)

            def norm1(b, j):
                act.wait_ge(ln1_scale, val(b, lambda t: t + 1))
                wait(act, d_full[1], val(b, lambda t: ordinal["xT1", t - 1] if t else 0))
                act.activation(xn[:, j, :], xin[b.par][:, j, :], ACT.Identity, bias=nmr[:, j:j + 1],
                               scale=rstd[:, j:j + 1]).then_inc(xn_ready, 1)

            def norm2(b, j):
                act.wait_ge(ln2_scale, val(b, lambda t: t + 1))
                wait(act, d_full[1], val(b, lambda t: ordinal["nT1", t - 1] if t else 0))
                wait(act, z_ready, val(b, lambda t: t))
                act.activation(x2[:, j, :], x1[:, j, :], ACT.Identity, bias=nmr2[:, j:j + 1],
                               scale=rstd2[:, j:j + 1]).then_inc(x2_ready, 1)

            def xT(b, c):
                src = full(act, b, f"xT{c}")
                wait(act, d_full[1], val(b, lambda t: ordinal["q1", t - 1] if t else 0))
                act.copy(xnT[:, c, :], src[:]).then_inc(d_free[c], 1)

            def q1(b, m):
                src = full(act, b, f"q{m}")
                wait(act, q_dram, val(b, lambda t: 48 * t))
                act.activation(qp[:, 0, m, :], src[:], ACT.Copy, scale=SCALE).then_inc(q1_ready, 1)

            def q2(b, m):
                act.wait_ge(qr_ready, val(b, lambda t: 2 * t + m + 1))
                act.copy(qp[:, 1, m, :], qr[:, m, :]).then_inc(q2_ready, 1)

            def k1(b, m):
                src = full(act, b, f"k{m}")
                wait(act, k_dram, val(b, lambda t: 48 * (t // 2)))
                if isinstance(b.i, int) and b.i == 0 and b.o == 0:
                    act.wait_ge(pool_cleared, 2)
                act.copy(kp[:, 0, m, 0:SK], src[:, 0:SK]).then_inc(k1_ready, 1)

            def k2(b, m):
                act.wait_ge(kr_ready, val(b, lambda t: 2 * (t // 2) + m + 1))
                act.copy(kp[:, 1, m, 0:SK], kr[:, m, :]).then_inc(k2_ready, 1)

            def v_main(part):
                v = v_n[:].rearrange("p g (h e) -> p g h e", e=VW)
                return v[:, :, 0:HG, HD * part:HD * part + HD]

            def v1(b, tail):
                src = full(act, b, f"v{tail}")
                for g in range(2):
                    wait(act, v_c_in[g], val(b, lambda t: 16 * (t // 2)))
                if isinstance(b.i, int) and b.i == 0 and b.o == 0:
                    act.wait_ge(dve_cleared, 2)
                if tail:
                    for q in range(4):
                        rows = slice(32 * q, 32 * q + 32)
                        ins = act.copy(v_tail(q, 0), vt_in(src[rows, 0:D], q))
                else:
                    for g in range(2):
                        ins = act.copy(v_main(0)[:, g], src[:, P * g:P * g + P].rearrange("p (h d) -> p h d", d=HD))
                ins.then_inc(v1_ready, 1)

            def vt_in(a, q):
                return a.rearrange("p (gg h d) -> p gg h d", gg=4, d=HD)[:, :, q, :]

            def v_tail(q, part):
                v = v_n[32 * q:32 * q + 32].rearrange("p g (a gg h e) -> p g a gg h e", a=2, gg=2, e=VW)
                return v[:, :, 1, :, q, HD * part:HD * part + HD]

            def v2(b, tail):
                act.wait_ge(vr_ready, val(b, lambda t: 2 * (t // 2) + tail + 1))
                if tail:
                    for q in range(4):
                        ins = act.copy(v_tail(q, 1), vt_in(vr[32 * q:32 * q + 32, 1, :], q))
                else:
                    for g in range(2):
                        ins = act.copy(v_main(1)[:, g], vr[:, 0, P * g:P * g + P].rearrange("p (h d) -> p h d", d=HD))
                ins.then_inc(v2_ready, 1)

            def max_rows(b, g):
                name = f"max{g}"
                src = full(act, b, name)
                wait(act, nm_rows[(b.par + 1) % 2][g], val(b, lambda t: 48 * ((t - 1) // 2 + 1) if t else 0))
                act.copy(nmT[g][:], src[0:3 * HG, 0:QB // 2].bitcast(BF16)).then_inc(d_free[bank_of[name]], 1)
                act.wait_ge(d_free[bank_of[name]], nth(b, name))
                for part in range(3):
                    act.dma_start(qst[b.par][NROW + part:NROW + part + 1, HG * g:HG * g + HG, :],
                                  nmT[g][HG * part:HG * part + HG, :]).then_inc(nm_rows[b.par][g], 16)

            def oT_out(b, c):
                src = full(act, b, f"oT{c}")
                wait(act, d_full[1], val(b, lambda t: ordinal["wo1", t - 1] if t else 0))
                act.copy(oT[:, c, :], src[:]).then_inc(d_free[c], 1)

            def nT_out(b, c):
                src = full(act, b, f"nT{c}")
                wait(act, d_full[0], val(b, lambda t: ordinal["down0", t - 1] if t else 0))
                act.copy(x2T[:, c, :], src[:]).then_inc(d_free[c], 1)

            def gate_exp(b, part=0):
                act.wait_ge(g_diff, val(b, lambda t: t // 2 + 1))
                act.activation(g_sel[:, 2, :], g_sel[:, 1, :], ACT.Exp).then_inc(g_exp, 1)

            def dn_out(b, part=0):
                src = full(act, b, "down0")
                act.wait_ge(g_col_ready, val(b, lambda t: t // 2 + 1))
                wait(act, d_full[0], val(b, lambda t: ordinal["up1", t - 1] if t else 0))
                act.activation(dn[:], src[:], ACT.Copy, scale=g_col[:, 0:1]).then_inc(d_free[0], 1)

            def store(b, part=0):
                act.wait_ge(y_ready, val(b, lambda t: 2 * (t + 1)))
                act.dma_start(out[bass.ds(b.row(), QB), :].rearrange("(j p) d -> p j d", p=P), y[:]
                              ).then_inc(y_out, 16)

            DO = {"exp": exps, "k1": k1, "k2": k2, "v1": v1, "v2": v2, "norm1_x": norm1, "xT": xT, "q1": q1, "q2": q2,
                  "oT": oT_out, "norm2_x": norm2, "nT": nT_out, "gexp": gate_exp, "down": dn_out, "max": max_rows,
                  "store": store}

            def stage(name, b):
                for part in parts(ACT_AT, name):
                    DO[name](b, part)

            b0 = Blk(0, 0)
            load_x(b0)
            load_ctx(b0)
            load_x(b0.at(1))
            for name, b, part in first_stages(ACT_FIRST, ACT_AT):
                DO[name](b, part)

            def slot(sl):
                if sl.has_project and sl.b.par == 0:
                    load_x(sl.b.at(2))
                    load_x(sl.b.at(3))
                if sl.has_kv:
                    load_ctx(sl.b.at(2))
                load_xres(sl.b)
                for name, b, part in sl.stages(ACT_AT):
                    DO[name](b, part)

            run(act, slot)
            last = Blk(NB, -1)
            for name in ("oT", "norm2_x", "nT", "down", "store"):
                stage(name, last)

        @block.vector
        def _(dve):
            STEPS = {"ln1b": NJ + 2, "ln2b": NJ + 2, "max": 4, "gate_a": 8, "gate_b": 3, "ln1a": 1, "ln2a": 1}
            order = [(name, b.o, part) for name, b, part in first_stages(DVE_FIRST, DVE_AT) if name in STEPS]
            for sl in slots():
                order += [(name, 2 * b.i + b.o, part) for name, b, part in sl.stages(DVE_AT) if name in STEPS]
            for name in ("ln2a", "ln2b"):
                order += [(name, NBLK - 1, part) for part in parts(DVE_AT, name)]
            done, total = {}, 0
            for name, t, part in order:
                done[f"{name}{part}", t] = total
                total += STEPS[name]

            def step(ins, b, name, n):
                ins.then_inc(dve_step, 1)
                if name.startswith("ln"):
                    hold(dve, dve_step, val(b, lambda t: done[name, t] + n))
                else:
                    dve.wait_ge(dve_step, val(b, lambda t: done[name, t] + n))

            def mark(ins):
                ins.then_inc(dve_step, 1)

            def first_guess(b, name, stats, mv, var, rstd, ready):
                hold(dve, dve_step, val(b, lambda t: done[name, t]))
                for j in range(NJ):
                    ins = dve.bn_aggr(mv[:, j, :], stats[:, j, :])
                    mark(ins) if j < NJ - 1 else step(ins, b, name, NJ)
                step(dve.tensor_scalar(var[:], mv[:, :, 1], EPS, None, ALU.add), b, name, NJ + 1)
                step(dve.tensor_single_scalar(rstd[:].bitcast(I32), var[:].bitcast(I32), 1,
                                              ALU.logical_shift_right), b, name, NJ + 2)
                dve.tensor_scalar(rstd[:].bitcast(I32), rstd[:].bitcast(I32), -1.0, RSQRT_BITS, ALU.mult, ALU.add
                                  ).then_inc(ready, 1)

            def ln1a(b, j):
                dve.wait_ge(x_in[b.par], val(b, lambda t: 16 * (t // 2 + 1)))
                mark(dve.bn_stats(stats[:, j, :], xin[b.par][:, j, :]))

            def ln1b(b, part):
                hold(dve, xn_ready, val(b, lambda t: NJ * t))
                first_guess(b, "ln1b0", stats, mv, var, rstd, ln1_stats)

            def ln2a(b, j):
                dve.wait_ge(x1_ready, val(b, lambda t: 2 * t + j // 2 + 1))
                mark(dve.bn_stats(stats2[:, j, :], x1[:, j, :]))

            def ln2b(b, part):
                hold(dve, x2_ready, val(b, lambda t: NJ * t))
                first_guess(b, "ln2b0", stats2, mv2, var2, rstd2, ln2_stats)

            def q_rest(b, m):
                dve.wait_ge(q1_ready, val(b, lambda t: 2 * t + m + 1))
                wait(dve, q3_ready, val(b, lambda t: 2 * t))
                wait(dve, q2_ready, val(b, lambda t: 2 * t))
                dve.scalar_tensor_tensor(qr[:, m, :], ps_d[m][:], SCALE, qp[:, 0, m, :], ALU.mult,
                                         ALU.subtract).then_inc(qr_ready, 1)
                dve.wait_ge(qr_ready, val(b, lambda t: 2 * t + m + 1))
                dve.sem_inc(d_free[m], 1)

            def q3(b, m):
                dve.wait_ge(q2_ready, val(b, lambda t: 2 * t + m + 1))
                dve.tensor_tensor(qp[:, 2, m, :], qr[:, m, :], qp[:, 1, m, :], ALU.subtract).then_inc(q3_ready, 1)

            def k_rest(b, m):
                dve.wait_ge(k1_ready, val(b, lambda t: 2 * (t // 2) + m + 1))
                wait(dve, k3_ready, val(b, lambda t: 2 * (t // 2)))
                dve.tensor_tensor(kr[:, m, :], ps_d[m][:, 0:SK], kp[:, 0, m, 0:SK], ALU.subtract
                                  ).then_inc(kr_ready, 1)
                dve.wait_ge(kr_ready, val(b, lambda t: 2 * (t // 2) + m + 1))
                dve.sem_inc(d_free[m], 1)

            def k3(b, m):
                dve.wait_ge(k2_ready, val(b, lambda t: 2 * (t // 2) + m + 1))
                dve.tensor_tensor(kp[:, 2, m, 0:SK], kr[:, m, :], kp[:, 1, m, 0:SK], ALU.subtract
                                  ).then_inc(k3_ready, 1)

            def heads(a):
                return a.rearrange("p (h d) -> p h d", d=HD)

            def v_main(g, part):
                return v_n[:, g, 0:HG * VW].rearrange("p (h e) -> p h e", e=VW)[:, :, HD * part:HD * part + HD]

            def v_tail(q, part):
                v = v_n[32 * q:32 * q + 32].rearrange("p g (a gg h e) -> p g a gg h e", a=2, gg=2, e=VW)
                return v[:, :, 1, :, q, HD * part:HD * part + HD]

            def vt_in(a, q):
                return a.rearrange("p (g gg h d) -> p g gg h d", g=2, gg=2, d=HD)[:, :, :, q, :]

            def v_rest(b, tail):
                dve.wait_ge(v1_ready, val(b, lambda t: 2 * (t // 2) + tail + 1))
                wait(dve, v3_ready, val(b, lambda t: 5 * (t // 2)))
                if tail:
                    for q in range(4):
                        r = slice(32 * q, 32 * q + 32)
                        ins = dve.tensor_tensor(vt_in(vr[r, 1, :], q), vt_in(ps_d[1][r, 0:D], q), v_tail(q, 0),
                                                ALU.subtract)
                else:
                    for g in range(2):
                        ins = dve.tensor_tensor(heads(vr[:, 0, P * g:P * g + P]), heads(ps_d[0][:, P * g:P * g + P]),
                                                v_main(g, 0), ALU.subtract)
                ins.then_inc(vr_ready, 1)
                dve.wait_ge(vr_ready, val(b, lambda t: 2 * (t // 2) + tail + 1))
                dve.sem_inc(d_free[tail], 1)

            def v3(b, tail):
                dve.wait_ge(v2_ready, val(b, lambda t: 2 * (t // 2) + tail + 1))
                if tail:
                    for q in range(4):
                        dve.tensor_tensor(v_tail(q, 2), vt_in(vr[32 * q:32 * q + 32, 1, :], q), v_tail(q, 1),
                                          ALU.subtract).then_inc(v3_ready, 1)
                    return
                for g in range(2):
                    ins = dve.tensor_tensor(v_main(g, 2), heads(vr[:, 0, P * g:P * g + P]), v_main(g, 1),
                                            ALU.subtract)
                ins.then_inc(v3_ready, 1)

            def maxima(b, u):
                kb, j = UNITS[u]
                n = min(HPB, H - HPB * kb)
                dve.wait_ge(s_full, val(b, lambda t: len(UNITS) * t + u + 1))
                dve.tensor_reduce(negm[:, j, HPB * kb:HPB * kb + n],
                                  ps_s[u % 2][:, 0:n * SK].rearrange("p (h k) -> p h k", k=SK),
                                  X, ALU.max, negate=True).then_inc(s_free, 1)

            def max_parts(b, g):
                name, hs = f"max{g}", slice(HG * g, HG * g + HG)
                dve.wait_ge(s_free, val(b, lambda t: len(UNITS) * t + (len(UNITS) if g else 3 * NJ)))
                k = bank_of[f"max{g}"]
                wait(dve, d_full[k], val(b, lambda t: ordinal[f"max{g}", t - 1] if t else 0))
                step(dve.tensor_scalar(nms[:], negm[:, :, hs], SHIFT, None, ALU.add), b, name, 1)
                step(dve.tensor_copy(nmp[g][:, :, 0, :], nms[:]), b, name, 2)
                step(dve.tensor_tensor(nmr1[:], nms[:], nmp[g][:, :, 0, :], ALU.subtract), b, name, 3)
                step(dve.tensor_copy(nmp[g][:, :, 1, :], nmr1[:]), b, name, 4)
                dve.tensor_tensor(nmp[g][:, :, 2, :], nmr1[:], nmp[g][:, :, 1, :], ALU.subtract
                                  ).then_inc(nmp_ready[g], 1)

            first_pb = [min(k for k in DVE_AT["pb"] if k // NT == g) for g in range(2)]

            def residual(b, k):
                g, kk, _, _ = tile_of(k)
                dve.wait_ge(t_done, val(b, lambda t: NK * t + k + 1))
                if k in first_pb:
                    wait(dve, o_full, val(b, lambda t: 2 * NJ * (t - 1) + NJ * (g + 1) if t else 0))
                dve.tensor_tensor(pb[g][:, kk, :], p32[:, k % NRING, :], pa[g][:, kk, :], ALU.subtract
                                  ).then_inc(pb_dve, 1)

            def sum_o(b, g, j):
                dve.wait_ge(o_full, val(b, lambda t: 2 * NJ * t + NJ * g + j + 1))
                wait(dve, on_ready, val(b, lambda t: max(0, 2 * NJ * t + NJ * g + j - 1)))
                o = ps_o[j % 2][:, 0:HG * VW].rearrange("p (h e) -> p h e", e=VW)
                dve.tensor_reduce(osum[:, j % 2], o[:, :, 0:3 * HD].rearrange("p h (x d) -> p h d x", x=3),
                                  X, ALU.add)
                dve.reciprocal(rden[:, j % 2], o[:, :, 3 * HD]).then_inc(o_free, 1)

            def add_x(b, p):
                dve.wait_ge(xres_in[b.par], val(b, lambda t: 16 * (t // 2 + 1)))
                wait(dve, z_ready, val(b, lambda t: t))
                src = full(dve, b, f"wo{p}")
                dve.tensor_tensor(x1[:, 2 * p:2 * p + 2, :], xres[b.par][:, 2 * p:2 * p + 2, :],
                                  src[:].rearrange("p (j d) -> p j d", j=2), ALU.add).then_inc(x1_ready, 1)
                dve.wait_ge(x1_ready, val(b, lambda t: 2 * t + p + 1))
                dve.sem_inc(d_free[p], 1)

            def gate_a(b, part=0):
                src = full(dve, b, "logit0")
                g = "gate_a0"
                dve.wait_ge(late_consts_in, 80)
                step(dve.tensor_copy(g_l[:], src[0:1, 0:E]), b, g, 1)
                dve.sem_inc(d_free[0], 1)
                l_j = g_l[:].unsqueeze(1).broadcast_to([1, E, E])
                l_e = g_l[:].unsqueeze(2).broadcast_to([1, E, E])
                mark(dve.tensor_tensor(g_eq[:], l_j, l_e, ALU.is_equal))
                mark(dve.tensor_tensor(g_gt[:], l_j, l_e, ALU.is_gt))
                step(dve.tensor_reduce(g_s[:, 0:1], g_l[:], X, ALU.max), b, g, 4)
                step(dve.tensor_tensor(g_eq[:], g_eq[:], tri_sb[:].rearrange("a (e j) -> a e j", j=E), ALU.mult),
                     b, g, 5)
                step(dve.tensor_tensor(g_gt[:], g_gt[:], g_eq[:], ALU.add), b, g, 6)
                step(dve.tensor_reduce(g_sel[:, 3, :], g_gt[:], X, ALU.add), b, g, 7)
                step(dve.tensor_single_scalar(g_sel[:, 0, :], g_sel[:, 3, :], 2.0, ALU.is_lt), b, g, 8)
                dve.tensor_scalar(g_sel[:, 1, :], g_l[:], g_s[:, 0:1], None, ALU.subtract).then_inc(g_diff, 1)

            def gate_b(b, part=0):
                g = "gate_b0"
                dve.wait_ge(g_exp, val(b, lambda t: t // 2 + 1))
                step(dve.tensor_tensor(g_sel[:, 4, :], g_sel[:, 2, :], g_sel[:, 0, :], ALU.mult), b, g, 1)
                step(dve.tensor_reduce(g_s[:, 1:2], g_sel[:, 4, :], X, ALU.add), b, g, 2)
                step(dve.reciprocal(g_s[:, 2:3], g_s[:, 1:2]), b, g, 3)
                dve.tensor_scalar(g_row[:], g_sel[:, 4, :].unsqueeze(2).broadcast_to([1, E, R]), g_s[:, 2:3], None,
                                  ALU.mult).then_inc(g_row_ready, 1)

            def gate_col(b, part=0):
                src = full(dve, b, "gcol0")
                wait(dve, d_free[0], val(b, lambda t: ordinal["down0", t - 1] if t else 0))
                dve.tensor_copy(g_col[:], src[:, 0:1]).then_inc(g_col_ready, 1)
                dve.wait_ge(g_col_ready, val(b, lambda t: t // 2 + 1))
                dve.sem_inc(d_free[1], 1)

            def add_z(b, p):
                dve.wait_ge(z_ready, val(b, lambda t: t + 1))
                wait(dve, y_out, val(b, lambda t: 16 * t))
                name = f"up{p}"
                src = full(dve, b, name)
                dve.tensor_tensor(y[:, 2 * p:2 * p + 2, :], z[:, 2 * p:2 * p + 2, :],
                                  src[:].rearrange("p (j d) -> p j d", j=2), ALU.add).then_inc(y_ready, 1)
                dve.wait_ge(y_ready, val(b, lambda t: 2 * t + p + 1))
                dve.sem_inc(d_free[bank_of[name]], 1)

            def sum0(b, j):
                sum_o(b, 0, j)

            def sum1(b, j):
                sum_o(b, 1, j)

            def open_masks(b, part):
                dve.wait_ge(masks_in, 96)
                for dst, src in ((maskq, m8), (maskk, mt8), (maskt, mtt8)):
                    dve.tensor_scalar(dst[:], src[:], -MASKED, MASKED, ALU.mult, ALU.add).then_inc(masks_ready, 1)

            def identity(b, part):
                dve.wait_ge(consts_in, 64)
                dve.tensor_copy(id16[:], id32[:]).then_inc(id16_ready, 1)

            DO = {"id16": identity, "masks": open_masks, "pb": residual, "sum0": sum0, "sum1": sum1, "unit": maxima, "max": max_parts, "kr": k_rest, "k3": k3,
                  "vr": v_rest, "v3": v3, "ln1a": ln1a, "ln1b": ln1b, "addx": add_x, "ln2a": ln2a, "ln2b": ln2b,
                  "qr": q_rest, "q3": q3, "gate_a": gate_a, "gate_b": gate_b, "gcol": gate_col, "y": add_z}

            def stage(name, b):
                for part in parts(DVE_AT, name):
                    DO[name](b, part)

            b0 = Blk(0, 0)
            dve.memset(v_n[:], 0.0).then_inc(v_zero, 1)
            dve.wait_ge(v_zero, 1)
            dve.memset(v_n[:, :, 0:HG * VW].rearrange("p g (h e) -> p g h e", e=VW)[:, :, :, VW - 1], 1.0
                       ).then_inc(dve_cleared, 1)
            for q in range(4):
                v = v_n[32 * q:32 * q + TAIL].rearrange("p g (a gg h e) -> p g a gg h e", a=2, gg=2, e=VW)
                ins = dve.memset(v[:, :, 1, :, q, VW - 1], 1.0)
            ins.then_inc(dve_cleared, 1)
            dve.memset(kst_n[NROW:NMAX], 1.0).then_inc(dve_cleared, 1)
            dve.memset(one1[:], 1.0).then_inc(one_ready, 1)
            for name, b, part in first_stages(DVE_FIRST, DVE_AT):
                DO[name](b, part)

            def slot(sl):
                for name, b, part in sl.stages(DVE_AT):
                    DO[name](b, part)

            run(dve, slot)
            last = Blk(NB, -1)
            for name in ("sum1", "addx", "ln2a", "ln2b", "y"):
                stage(name, last)

        @block.tensor
        def _(pe):
            def project_k(b, m):
                pe.wait_ge(ctx_in, val(b, lambda t: 16 * (t // 2 + 1)))
                dst = fill(pe, b, f"k{m}")
                for c in range(KC):
                    mm = pe.matmul(dst[:, 0:SK], wk[:, c, P * m:P * m + P], cin[:, c, :],
                                   start=c == 0, stop=c == KC - 1)
                mm.then_inc(d_full[m], 1)

            def project_v(b, tail):
                if tail:
                    pe.wait_ge(tail_copied, val(b, lambda t: t // 2 + 1))
                else:
                    pe.wait_ge(ctx_in, val(b, lambda t: 16 * (t // 2 + 1)))
                dst = fill(pe, b, f"v{tail}")
                for c in range(KC):
                    keys = ctail[:, c].rearrange("p q k -> p (q k)") if tail else cin[:, c, 0:P]
                    mm = pe.matmul(dst[:, 0:D], keys, wv[:, c, :], start=c == 0, stop=c == KC - 1)
                mm.then_inc(d_full[tail], 1)

            def turn(b, name, src, c):
                dst = fill(pe, b, f"{name}{c}")
                for j in range(NJ):
                    mm = pe.transpose(dst[:, P * j:P * j + P], src[:, j, P * c:P * c + P], id32[:])
                mm.then_inc(d_full[c], 1)

            def turn_x(b, c):
                pe.wait_ge(xn_ready, val(b, lambda t: NJ * (t + 1)))
                turn(b, "xT", xn, c)

            def turn_o(b, c):
                pe.wait_ge(on_ready, val(b, lambda t: 2 * NJ * (t + 1)))
                turn(b, "oT", on, c)

            def turn_n(b, c):
                pe.wait_ge(x2_ready, val(b, lambda t: NJ * (t + 1)))
                turn(b, "nT", x2, c)

            def project_q(b, m):
                for c in range(KC):
                    pe.wait_ge(d_free[c], nth(b, f"xT{c}"))
                dst = fill(pe, b, f"q{m}")
                for c in range(KC):
                    mm = pe.matmul(dst[:], wq[:, c, P * m:P * m + P], xnT[:, c, :], start=c == 0,
                                   stop=c == KC - 1)
                mm.then_inc(d_full[m], 1)

            def score_unit(b, u):
                kb, j = UNITS[u]
                h0 = HPB * kb
                n = min(HPB, H - h0)
                keys = kst_c if b.par else kst_n
                if u == 0:
                    if b.par == 0:
                        pe.wait_ge(kst_n_in, val(b, lambda t: 48 * (t // 2 + 1)))
                    pe.wait_ge(q_stack[b.par][0], val(b, lambda t: 48 * (t // 2 + 1)))
                if b.par and kb in (0, 2) and j == 0:
                    pe.wait_ge(kst_c_in[kb // 2], val(b, lambda t: 16 * (t // 2 + 1)))
                if kb == 2 and j == 0:
                    pe.wait_ge(q_stack[b.par][1], val(b, lambda t: 48 * (t // 2 + 1)))
                wait(pe, s_free, val(b, lambda t: max(0, len(UNITS) * t + u - 1)))
                dst = ps_s[u % 2]
                pe.matmul(dst[:, 0:n * SK].rearrange("p (h k) -> p h k", k=SK), id16[:],
                          maskq[:, NJ * b.par + j, :].unsqueeze(1).broadcast_to([P, n, SK]),
                          start=True, stop=False, skip_group_check=True)
                for h in range(n):
                    mm = pe.matmul(dst[:, h * SK:(h + 1) * SK], qst[b.par][0:NROW, h0 + h, P * j:P * j + P],
                                   keys[0:NROW, h0 + h, 0:SK], start=False, stop=h == n - 1,
                                   skip_group_check=True)
                mm.then_inc(s_full, 1)

            def score_tile(b, k):
                g, kk, gg, hq = tile_of(k)
                if kk == 0:
                    pe.wait_ge(nm_rows[b.par][g], val(b, lambda t: 48 * (t // 2 + 1)))
                    pe.wait_ge(kst_c_in[g], val(b, lambda t: 16 * (t // 2 + 1)))
                wait(pe, t_done, val(b, lambda t: max(0, NK * t + k - 1)))
                dst = ps_t[k % 2]
                h0 = HG * g + 4 * gg
                cols = slice(QB * b.par, QB * b.par + QB)
                if hq < 4:
                    pe.matmul(dst[:], kst_c[:, h0 + hq, 0:P], qst[b.par][:, h0 + hq, :], start=True, stop=False)
                    pe.matmul(dst[:], id16[:], maskk[:, cols], start=False, stop=True).then_inc(t_full, 1)
                    return
                for q in range(4):
                    pe.matmul(dst[32 * q:32 * q + 32, :], kst_c[:, h0 + q, P:SKP], qst[b.par][:, h0 + q, :],
                              start=True, stop=False, skip_group_check=True)
                pe.matmul(dst[:], id16[:], maskt[:, cols], start=False, stop=True,
                          skip_group_check=True).then_inc(t_full, 1)

            def pv(b, g, j):
                if j == 0:
                    pe.wait_ge(pb_dve, val(b, lambda t: pb_count(NK * t + NT * (g + 1), False)))
                    pe.wait_ge(pb_pool, val(b, lambda t: pb_count(NK * t + NT * (g + 1), True)))
                    pe.wait_ge(v_c_in[g], val(b, lambda t: 16 * (t // 2 + 1)))
                wait(pe, o_free, val(b, lambda t: max(0, 2 * NJ * t + NJ * g + j - 1)))
                dst = ps_o[j % 2]
                first = True
                for half, part in enumerate((pa[g], pb[g])):
                    for kk in range(NT):
                        gg, hq = divmod(kk, 5)
                        if hq < 4:
                            at, w, v = (4 * gg + hq) * VW, VW, (4 * gg + hq) * VW
                        else:
                            at, w, v = 4 * gg * VW, 4 * VW, (HG + 4 * gg) * VW
                        mm = pe.matmul(dst[:, at:at + w], part[:, kk, P * j:P * j + P], v_c[:, g, v:v + w],
                                       start=first, stop=half == 1 and kk == NT - 1, skip_group_check=True)
                        first = False
                mm.then_inc(o_full, 1)

            def pv0(b, j):
                pv(b, 0, j)

            def pv1(b, j):
                pv(b, 1, j)

            def apply_wo(b, p):
                for c in range(KC):
                    pe.wait_ge(d_free[c], nth(b, f"oT{c}"))
                pe.wait_ge(late_consts_in, 80)
                dst = fill(pe, b, f"wo{p}")
                for j in range(2):
                    for c in range(KC):
                        mm = pe.matmul(dst[:, D * j:D * j + D], oT[:, c, P * (2 * p + j):P * (2 * p + j) + P],
                                       wo[:, c, :], start=c == 0, stop=c == KC - 1, skip_group_check=True)
                mm.then_inc(d_full[p], 1)

            def logits(b, part=0):
                for c in range(KC):
                    pe.wait_ge(d_free[c], nth(b, f"nT{c}"))
                dst = fill(pe, b, "logit0")
                for c in range(KC):
                    mm = pe.matmul(dst[0:1, 0:E], x2T[:, c, 0:1], wrout[:, c, :], start=c == 0, stop=c == KC - 1)
                mm.then_inc(d_full[0], 1)

            def gate_col(b, part=0):
                pe.wait_ge(one_ready, 1)
                pe.wait_ge(g_row_ready, val(b, lambda t: t // 2 + 1))
                dst = fill(pe, b, "gcol0")
                pe.matmul(dst[:, 0:1], g_row[:].rearrange("a e r -> a (e r)"), one1[:], start=True, stop=True
                          ).then_inc(d_full[1], 1)

            def down(b, part=0):
                for c in range(KC):
                    pe.wait_ge(d_free[c], nth(b, f"nT{c}"))
                dst = fill(pe, b, "down0")
                for c in range(KC):
                    mm = pe.matmul(dst[:], wdown[:, c, :], x2T[:, c, :], start=c == 0, stop=c == KC - 1)
                mm.then_inc(d_full[0], 1)

            def up(b, p):
                pe.wait_ge(d_free[0], nth(b, "down0"))
                name = f"up{p}"
                dst = fill(pe, b, name)
                for j in range(2):
                    mm = pe.matmul(dst[:, D * j:D * j + D], dn[:, P * (2 * p + j):P * (2 * p + j) + P], wup[:],
                                   start=True, stop=True, skip_group_check=True)
                mm.then_inc(d_full[bank_of[name]], 1)

            def max_turn(b, g):
                dst = fill(pe, b, f"max{g}")
                hold(pe, nmp_ready[g], val(b, lambda t: t + 1))
                for j in range(NJ):
                    mm = pe.transpose(dst[0:3 * HG, 64 * j:64 * j + 64].bitcast(BF16),
                                      nmp[g][:, j].rearrange("p a h -> p (a h)"), id16[:])
                mm.then_inc(d_full[bank_of[f"max{g}"]], 1)

            DO = {"tile": score_tile, "pv0": pv0, "pv1": pv1, "unit": score_unit, "k": project_k, "v": project_v,
                  "oT": turn_o, "wo": apply_wo, "xT": turn_x, "q": project_q, "nT": turn_n, "logit": logits,
                  "gcol": gate_col, "down": down, "up": up, "max": max_turn}

            def stage(name, b):
                for part in parts(PE_AT, name):
                    DO[name](b, part)

            pe.wait_ge(consts_in, 64)
            for name, b, part in first_stages(PE_FIRST, PE_AT):
                if name == "unit" and part == 0:
                    pe.wait_ge(id16_ready, 1)
                    pe.wait_ge(masks_ready, 3)
                DO[name](b, part)

            def slot(sl):
                for name, b, part in sl.stages(PE_AT):
                    DO[name](b, part)

            run(pe, slot)
            last = Blk(NB, -1)
            for name in ("pv1", "oT", "wo", "nT", "down", "up"):
                stage(name, last)


def kernel(x, ctx_1024, mask_1x1xSxS2_bk0, L0_xattn_W_q, L0_xattn_W_k, L0_xattn_W_v, L0_xattn_W_o,
           L0_ffn_router_w, L0_ffn_lora_down, L0_ffn_lora_up):
    import numpy as np
    import concourse.bacc as bacc
    from concourse.bass_utils import run_bass_kernel_spmd

    def laid(a):
        return np.ascontiguousarray(a)

    def by_pairs(w):
        return laid(np.asarray(w).T.reshape(D, H // 2, 2, HD).transpose(0, 2, 1, 3).reshape(D, D))

    mask2 = np.asarray(mask_1x1xSxS2_bk0).reshape(S, SK)
    arrays = {
        "x": laid(np.asarray(x).reshape(NB * S, D)),
        "ctxT": laid(np.asarray(ctx_1024).transpose(0, 2, 1)),
        "mask": laid(mask2),
        "maskT": laid(mask2.T),
        "wqT": by_pairs(L0_xattn_W_q),
        "wkT": by_pairs(L0_xattn_W_k),
        "wvT": laid(np.asarray(L0_xattn_W_v).T),
        "woT": laid(np.asarray(L0_xattn_W_o).T),
        "routerT": laid(np.asarray(L0_ffn_router_w).T),
        "downT": laid(np.asarray(L0_ffn_lora_down).reshape(E * R, D).T),
        "upT": laid(np.asarray(L0_ffn_lora_up).transpose(0, 2, 1).reshape(E * R, D)),
        "ident": np.eye(P, dtype=np.float32),
        "tri": np.tril(np.ones((E, E), np.float32), -1).reshape(1, E * E),
    }
    nc = bacc.Bacc("TRN2", target_bir_lowering=False, num_devices=1)
    args = [nc.dram_tensor(n, a.shape, mybir.dt.from_np(a.dtype), kind="ExternalInput").ap()
            for n, a in arrays.items()]
    out = nc.dram_tensor("out", (NB * S, D), F32, kind="ExternalOutput").ap()
    build(nc, *args, out)
    r = run_bass_kernel_spmd(nc, [arrays], core_ids=[0])
    return r.results[0]["out"].reshape(NB, S, D)
```

```python
from contextlib import ExitStack

import concourse.bass as bass
from concourse import mybir

F32 = mybir.dt.float32
BF16 = mybir.dt.bfloat16
F16 = mybir.dt.float16
U8 = mybir.dt.uint8
I32 = mybir.dt.int32
ALU = mybir.AluOpType
ACT = mybir.ActivationFunctionType
X = mybir.AxisListType.X

D, H, HD = 256, 16, 16
NB, S, SK = 4, 1024, 154
E, R = 8, 16
P = 128
QB = 512
NJ = QB // P
NBLK = NB * S // QB
KC = D // P
TAIL = SK - P
SKP = P + 32
QSLOTS = ((0, 0, 3), (1, 3, 2), (2, 5, 1))
KSLOTS = ((0, 3), (3, 2), (5, 1))
NROW = 6 * HD
NMAX = NROW + 3
VW = 1 + 3 * HD
VWB = 1 + 2 * HD
HG = H // 2
VG = 2 * HG * VW
NT = 10
NK = 2 * NT
HPB = 3
NU = (H + HPB - 1) // HPB
MASKED = -float(2 ** 99)
LOWEST = -3.0e38
SHIFT = 9.704060527839234
EPS = 1e-5
NRING = 4
RSQRT_BITS = float(0x5F3759DF)
NEWTON = 3
LN_STEPS = 5 + 3 * NEWTON
MAX_STEPS = 5
SCALE = 0.25


PE_AT = {
    "tile": tuple(range(NK)),
    "pv1": (0.13, 0.25, 0.65, 1.77),
    "pv0": (13.37, 15.37, 17.37, 18.48),
    "unit": (0.38, 1.38, 2.54, 3.54, 4.78, 5.24, 7.33, 7.46, 8.3, 8.59, 9.54, 9.69, 9.93, 11.1, 11.4, 12.48,
        12.66, 13.66, 13.92, 15.22, 15.52, 17.04, 17.51, 17.74),
    "k": (3.01, 4.38),
    "v": (4.56, 4.62),
    "oT": (5.19, 6.51),
    "wo": (7.42, 7.61),
    "xT": (9.57, 9.68),
    "max": (12.55, 19.95),
    "q": (11.05, 11.06),
    "nT": (13.88, 14.73),
    "logit": 14.75,
    "gcol": 18.79,
    "down": (15.83, 19.95),
    "up": (19.95, 19.95),
}
ACT_AT = {
    "exp": tuple(range(NK)),
    "k1": (2.23, 2.52),
    "k2": (4.71, 5.63),
    "v1": (3.02, 4.01),
    "v2": (8.59, 10.16),
    "oT": (5.66, 5.75),
    "norm1_x": (5.77, 7.12, 7.81, 8.14),
    "xT": (9.73, 9.93),
    "norm2_x": (10.3, 10.66, 11.07, 11.39),
    "max": (12.98, 19.94),
    "q1": (10.68, 11.12),
    "q2": (12.25, 12.55),
    "nT": (13.9, 15.05),
    "gexp": 16.52,
    "down": (18.47, 19.58),
}
DVE_AT = {
    "pb": {5: 7.21, 19: 19.95},
    "sum1": (0.02, 0.02, 0.51, 2.52),
    "sum0": (16.65, 16.95, 19.55, 19.95),
    "unit": (0.46, 1.46, 2.54, 3.54, 4.62, 5.24, 7.25, 7.43, 8.3, 8.57, 9.28, 9.49, 9.69, 10.88, 11.13, 11.96,
        12.48, 13.12, 13.33, 15.38, 15.47, 16.96, 17.64, 18.04),
    "kr": (3.51, 3.53),
    "k3": (9.92, 10.42),
    "vr": (3.66, 4.45),
    "v3": (10.01, 12.09),
    "ln1a": (0.8, 0.91, 1.11, 1.6),
    "ln1b": (3.22, 3.225, 3.4, 3.405, 3.54, 3.55, 3.555, 3.57, 3.575, 3.6, 3.71, 3.72, 4.27, 4.48),
    "addx": (7.39, 7.74),
    "ln2a": (7.39, 7.57, 7.85, 8.73),
    "ln2b": (9.355, 9.36, 9.365, 9.37, 9.375, 9.38, 9.385, 9.39, 9.395, 9.4, 9.405, 9.48, 9.485, 9.49),
    "max": (9.88, 9.89, 10.27, 10.28, 11.05, 18.67, 18.73, 18.77, 18.87, 19.84),
    "qr": (10.15, 10.95),
    "q3": (12.03, 14.45),
    "gate_a": 14.99,
    "gate_b": 17.16,
    "gcol": 18.18,
    "y": (19.95, 19.95),
}
POOL_AT = {
    "pb": {0: 1.36, 1: 2.47, 2: 3.38, 3: 4.41, 4: 5.68, 6: 7.38, 7: 8.68, 8: 9.38, 9: 10.38, 10: 11.35, 11:
        12.29, 12: 13.38, 13: 14.92, 14: 15.68, 15: 16.38, 16: 17.38, 17: 19.08, 18: 19.38},
    "o_norm1": (0.54, 0.54, 0.54, 0.54),
    "o_norm0": (17.14, 19.55, 19.6, 19.6),
    "tail": 1.52,
    "z": 14.06,
}
MASKED_BY_PE = (0, 1, 2, 3, 4, 7, 8, 9, 10, 11, 12, 14, 15, 16, 20, 21, 22, 23)
PE_FIRST = (
    ("k", 0), ("xT", 0), ("q", 0), ("v", 0), ("unit", 0, range(0, 6)), ("xT", 1), ("unit", 0, range(6, 12)),
    ("unit", 0, range(12, 18)), ("q", 1), ("unit", 0, range(18, 24)), ("max", 0, range(0, 1)), ("max", 0,
    range(1, 2)),
)
ACT_FIRST = (
    ("norm1_x", 0), ("k1", 0), ("k2", 0), ("xT", 0), ("q1", 0), ("v1", 0), ("q2", 0), ("norm1_x", 1), ("v2", 0),
    ("xT", 1), ("q1", 1), ("q2", 1), ("max", 0, range(0, 1)), ("max", 0, range(1, 2)),
)
DVE_FIRST = (
    ("ln1a", 0), ("ln1b", 0), ("kr", 0), ("k3", 0), ("ln1a", 1), ("qr", 0), ("id16", 0), ("q3", 0), ("vr", 0),
    ("ln1b", 1), ("masks", 0), ("v3", 0), ("unit", 0, range(0, 6)), ("unit", 0, range(6, 12)), ("unit", 0,
    range(12, 18)), ("qr", 1), ("q3", 1), ("max", 0, range(0, 5)), ("unit", 0, range(18, 24)), ("max", 0,
    range(5, 10)),
)
PE_LAST = (
    ("pv1", 0, range(0, 3)), ("pv1", 0, range(3, 4)), ("oT", 0, range(0, 1)), ("oT", 0, range(1, 2)), ("wo", 0,
    range(0, 1)), ("wo", 0, range(1, 2)), ("nT", 0, range(0, 1)), ("nT", 0, range(1, 2)), ("down", 0, range(0,
    1)), ("down", 0, range(1, 2)), ("up", 0),
)
ACT_LAST = (
    ("oT", 0), ("norm2_x", 0, range(0, 2)), ("norm2_x", 0, range(2, 4)), ("nT", 0, range(0, 1)), ("nT", 0,
    range(1, 2)), ("down", 0),
)
DVE_LAST = (
    ("sum1", 0), ("addx", 0, range(0, 1)), ("ln2a", 0, range(0, 2)), ("addx", 0, range(1, 2)), ("ln2a", 0,
    range(2, 4)), ("ln2b", 0), ("y", 0),
)
KV_STAGES = ("k", "v", "k1", "k2", "v1", "v2", "kr", "k3", "vr", "v3", "tail")
PROJECT_STAGES = ("xT", "q", "norm1_x", "q1", "q2", "ln1a", "ln1b", "qr", "q3")
MAXIMA_STAGES = ("unit", "max")
ATTEND_STAGES = ("tile", "exp", "pb", "pv0", "sum0", "o_norm0")
GATE_STAGES = ("logit", "gcol", "gexp", "gate_a", "gate_b")


class Blk:

    def __init__(self, i, o):
        self.i, self.o, self.par = i, o, o % 2

    def at(self, d):
        return Blk(self.i, self.o + d)

    def row(self):
        return self.i * (2 * QB) + self.o * QB


def build(nc, x, ctxT, mask, maskT, wqT, wkT, wvT, woT, routerT, downT, upT, ident, tri, out):
    with ExitStack() as es:
        def sb(name, shape, dt=F32):
            return es.enter_context(nc.sbuf_tensor(name, shape, dt))

        def psum(name):
            return es.enter_context(nc.psum_tensor(name, [P, 512], F32))

        def sem(name):
            return es.enter_context(nc.semaphore(name))

        wq, wk, wv, wo = (sb(n, [P, KC, D]) for n in ("wq", "wk", "wv", "wo"))
        wdown = sb("wdown", [P, KC, E * R])
        wup = sb("wup", [P, D])
        wrout = sb("wrout", [P, KC, E])
        id32 = sb("id32", [P, P])
        id16 = sb("id16", [P, P], BF16)
        tri_sb = sb("tri_sb", [1, E * E])
        one1 = sb("one1", [1, 1])
        m8 = sb("m8", [P, S // P, SK], U8)
        mt8 = sb("mt8", [P, S], U8)
        mtt8 = sb("mtt8", [P, S], U8)
        maskq = sb("maskq", [P, S // P, SK], BF16)
        maskk = sb("maskk", [P, S], BF16)
        maskt = sb("maskt", [P, S], BF16)
        cin = sb("cin", [P, KC, SK])
        ctail = sb("ctail", [P, KC, 4, 32])
        kp = sb("kp", [P, 3, 2, SKP], BF16)
        kr = sb("kr", [P, 2, SK])
        kst_n = sb("kst_n", [NMAX, H, SKP], BF16)
        kst_c = sb("kst_c", [NMAX, H, SKP], BF16)
        v_n = sb("v_n", [P, 2, VG], BF16)
        v_c = sb("v_c", [P, 2, VG], BF16)
        vr = sb("vr", [P, 2, D])
        kdram = nc.dram_tensor("kdram", [3, HD, H, SKP], BF16).ap()
        qdram = nc.dram_tensor("qdram", [3, HD, H, QB], BF16).ap()
        xin = [sb(f"xin{s}", [P, NJ, D]) for s in range(2)]
        xres = [sb(f"xres{s}", [P, NJ, D]) for s in range(2)]
        stats = sb("stats", [P, NJ, 6])
        mv = sb("mv", [P, NJ, 2])
        rstd = sb("rstd", [P, NJ])
        nmr = sb("nmr", [P, NJ])
        stats2 = sb("stats2", [P, NJ, 6])
        mv2 = sb("mv2", [P, NJ, 2])
        rstd2 = sb("rstd2", [P, NJ])
        nmr2 = sb("nmr2", [P, NJ])
        var = sb("var", [P, NJ])
        var2 = sb("var2", [P, NJ])
        newt = sb("newt", [P, NJ])
        newt2 = sb("newt2", [P, NJ])
        xn = sb("xn", [P, NJ, D])
        xnT = sb("xnT", [P, KC, QB])
        qp = sb("qp", [P, 3, 2, QB], BF16)
        qr = sb("qr", [P, 2, QB])
        qst = [sb(f"qst{s}", [NMAX, H, QB], BF16) for s in range(2)]
        smax = sb("smax", [P, NJ, H])
        masked = sb("masked", [P, 2, HPB, SK])
        nms = sb("nms", [P, NJ, HG])
        nmp = [sb(f"nmp{g}", [P, NJ, 3, HG], BF16) for g in range(2)]
        nmr1 = sb("nmr1", [P, NJ, HG])
        nmT = [sb(f"nmT{g}", [3 * HG, QB], BF16) for g in range(2)]
        p32 = sb("p32", [P, NRING, QB])
        pa = [sb(f"pa{g}", [P, NT, QB], F16) for g in range(2)]
        pb = [sb(f"pb{g}", [P, NT, QB], F16) for g in range(2)]
        osum = sb("osum", [P, 2, HG, HD])
        rden = sb("rden", [P, 2, HG])
        on = sb("on", [P, NJ, D])
        oT = sb("oT", [P, KC, QB])
        x1 = sb("x1", [P, NJ, D])
        x2 = sb("x2", [P, NJ, D])
        z = sb("z", [P, NJ, D])
        x2T = sb("x2T", [P, KC, QB])
        dn = sb("dn", [P, QB])
        y = sb("y", [P, NJ, D])
        g_l = sb("g_l", [1, E])
        g_eq = sb("g_eq", [1, E, E])
        g_gt = sb("g_gt", [1, E, E])
        g_sel = sb("g_sel", [1, 8, E])
        g_s = sb("g_s", [1, 4])
        g_row = sb("g_row", [1, E, R])
        g_col = sb("g_col", [P, 1])

        ps_s = [psum(f"ps_s{k}") for k in range(2)]
        ps_t = [psum(f"ps_t{k}") for k in range(2)]
        ps_o = [psum(f"ps_o{k}") for k in range(2)]
        ps_d = [psum(f"ps_d{k}") for k in range(2)]

        passed = sem("passed")
        consts_in = sem("consts_in")
        late_consts_in = sem("late_consts_in")
        masks_in = sem("masks_in")
        pool_cleared = sem("pool_cleared")
        dve_cleared = sem("dve_cleared")
        id16_ready = sem("id16_ready")
        masks_ready = sem("masks_ready")
        ctx_in = sem("ctx_in")
        tail_copied = sem("tail_copied")
        x_in = [sem(f"x_in{s}") for s in range(2)]
        xres_in = [sem(f"xres_in{s}") for s in range(2)]
        dve_step = sem("dve_step")
        ctail_cleared = sem("ctail_cleared")
        d_full = [sem(f"d_full{k}") for k in range(2)]
        d_free = [sem(f"d_free{k}") for k in range(2)]
        ln1_scale = sem("ln1_scale")
        ln2_scale = sem("ln2_scale")
        xn_ready = sem("xn_ready")
        q1_ready = sem("q1_ready")
        qr_ready = sem("qr_ready")
        q2_ready = sem("q2_ready")
        q3_ready = sem("q3_ready")
        q_dram = sem("q_dram")
        q_stack = [[sem(f"q_stack{s}{g}") for g in range(2)] for s in range(2)]
        v_zero = sem("v_zero")
        k1_ready = sem("k1_ready")
        kr_ready = sem("kr_ready")
        k2_ready = sem("k2_ready")
        k3_ready = sem("k3_ready")
        k_dram = sem("k_dram")
        kst_n_in = sem("kst_n_in")
        kst_c_in = [sem(f"kst_c_in{g}") for g in range(2)]
        v1_ready = sem("v1_ready")
        vr_ready = sem("vr_ready")
        v2_ready = sem("v2_ready")
        v3_ready = sem("v3_ready")
        v_c_in = [sem(f"v_c_in{g}") for g in range(2)]
        s_full = sem("s_full")
        s_free = sem("s_free")
        nmp_ready = [sem(f"nmp_ready{g}") for g in range(2)]
        nm_rows = [[sem(f"nm_rows{s}{g}") for g in range(2)] for s in range(2)]
        t_full = sem("t_full")
        t_done = sem("t_done")
        pb_dve = sem("pb_dve")
        pb_pool = sem("pb_pool")
        o_full = sem("o_full")
        o_free = sem("o_free")
        on_ready = sem("on_ready")
        x1_ready = sem("x1_ready")
        x2_ready = sem("x2_ready")
        z_ready = sem("z_ready")
        g_diff = sem("g_diff")
        g_exp = sem("g_exp")
        g_row_ready = sem("g_row_ready")
        one_ready = sem("one_ready")
        g_col_ready = sem("g_col_ready")
        y_ready = sem("y_ready")
        y_out = sem("y_out")

        def val(b, f):
            if isinstance(b.i, int):
                return f(2 * b.i + b.o)
            at1, at2 = f(2 + b.o), f(4 + b.o)
            return b.i * (at2 - at1) + (2 * at1 - at2)

        def wait(eng, s, v):
            if not isinstance(v, int) or v > 0:
                eng.wait_ge(s, v)

        def hold(eng, s, v):
            wait(eng, s, v)
            eng.sem_inc(passed, 1)

        class Slot:
            def __init__(self, b, first, last):
                self.b = b
                self.has_finish = not (first and b.par == 0)
                self.has_project = not last
                self.has_maxima = not (last and b.par == 1)
                self.has_kv = not last and b.par == 0
                self.nxt, self.prj, self.fin = b.at(1), b.at(2), b.at(-1)

            def stages(self, table):
                at = []
                for name, pos in table.items():
                    if not isinstance(pos, dict):
                        pos = dict(enumerate(pos if isinstance(pos, tuple) else (pos,)))
                    at += [(p, name, part) for part, p in pos.items()]
                for _, name, part in sorted(at):
                    if name in ATTEND_STAGES:
                        yield name, self.b, part
                    elif name in KV_STAGES:
                        if self.has_kv:
                            yield name, self.prj, part
                    elif name in PROJECT_STAGES:
                        if self.has_project:
                            yield name, self.prj, part
                    elif name in MAXIMA_STAGES:
                        if self.has_maxima:
                            yield name, self.nxt, part
                    elif self.has_finish and (name not in GATE_STAGES or self.fin.par == 0):
                        yield name, self.fin, part

        def parts(table, name):
            return range(len(table[name]) if name in table and isinstance(table[name], tuple) else 1)

        def listed(order, table, b0):
            for name, t, *some in order:
                for part in some[0] if some else parts(table, name):
                    yield name, b0.at(t), part

        FIRST, LAST = Blk(0, 0), Blk(NB, -1)

        def slots():
            for b in range(NB):
                for par in range(2):
                    yield Slot(Blk(b, par), b == 0, b == NB - 1)

        BANKS = {"k": (0, 1), "v": (0, 1), "xT": (0, 1), "q": (0, 1), "oT": (0, 1), "wo": (0, 1),
                 "nT": (0, 1), "logit": (0,), "gcol": (1,), "down": (0, 1), "up": (0, 1), "max": (0, 1)}
        uses = [(name, b.o, part) for name, b, part in listed(PE_FIRST, PE_AT, FIRST) if name in BANKS]
        for sl in slots():
            uses += [(name, 2 * b.i + b.o, part) for name, b, part in sl.stages(PE_AT) if name in BANKS]
        uses += [(name, NBLK - 1, part) for name, _, part in listed(PE_LAST, PE_AT, LAST) if name in BANKS]
        ordinal, bank_of, seen = {}, {}, [0, 0]
        for name, t, part in uses:
            bank = BANKS[name][part]
            seen[bank] += 1
            ordinal[f"{name}{part}", t] = seen[bank]
            bank_of[f"{name}{part}"] = bank

        def nth(b, name):
            return val(b, lambda t: ordinal[name, t])

        def fill(pe, b, name):
            k = bank_of[name]
            wait(pe, d_free[k], val(b, lambda t: ordinal[name, t] - 1))
            return ps_d[k]

        def full(eng, b, name):
            k = bank_of[name]
            eng.wait_ge(d_full[k], nth(b, name))
            return ps_d[k]

        def pb_count(n, on_pool):
            whole, rest = divmod(n, NK)
            mine = (POOL_AT if on_pool else DVE_AT)["pb"]
            return whole * len(mine) + sum(k < rest for k in mine)

        def tile_of(k):
            g, kk = divmod(k, NT)
            return g, kk, kk // 5, kk % 5

        def run(eng, slot):
            for s in range(2):
                slot(Slot(Blk(0, s), True, False))
            with eng.Fori(1, NB - 1) as i:
                for s in range(2):
                    slot(Slot(Blk(i, s), False, False))
            for s in range(2):
                slot(Slot(Blk(NB - 1, s), False, True))

        UNITS = [(kb, j) for kb in range(NU) for j in range(NJ)]

        block = es.enter_context(nc.Block())

        @block.sync
        def _(sp):
            def spread(part, src, dram, done):
                for_pairs = dram[part].rearrange("d (hh m) n -> hh d (m n)", m=2)
                sp.dma_start(for_pairs, src[:, part].rearrange("p m n -> p (m n)")).then_inc(done, 16)

            def q_to_dram(b):
                for g in range(2):
                    hold(sp, q_stack[(b.par + 1) % 2][g], val(b, lambda t: 48 * ((t - 1) // 2 + 1) if t else 0))
                for part, ready in enumerate((q1_ready, q2_ready, q3_ready)):
                    hold(sp, ready, val(b, lambda t: 2 * (t + 1)))
                    spread(part, qp, qdram, q_dram)

            def stack_q(b, g):
                hs = slice(HG * g, HG * g + HG)
                hold(sp, q_dram, val(b, lambda t: 48 * (t + 1)))
                hold(sp, t_full, val(b, lambda t: NK * (t - 2) + NT * (g + 1) if t >= 2 else 0))
                for part, to, n in QSLOTS:
                    sp.dma_start(qst[b.par][HD * to:HD * (to + n), hs, :],
                                 qdram[part, :, hs].unsqueeze(0).broadcast_to([n, HD, HG, QB])
                                 ).then_inc(q_stack[b.par][g], 16)

            def stack_k(b):
                for part, ready in enumerate((k1_ready, k2_ready, k3_ready)):
                    hold(sp, ready, val(b, lambda t: 2 * (t // 2 + 1)))
                    spread(part, kp, kdram, k_dram)
                hold(sp, s_full, val(b, lambda t: len(UNITS) * (t - 1) if t else 0))
                for g in range(2):
                    hold(sp, kst_c_in[g], val(b, lambda t: 16 * (t // 2)))
                hold(sp, k_dram, val(b, lambda t: 48 * (t // 2 + 1)))
                for to, n in KSLOTS:
                    sp.dma_start(kst_n[HD * to:HD * (to + n)], kdram[0:n]).then_inc(kst_n_in, 16)

            def keys_to_attend(b, g):
                hold(sp, kst_n_in, val(b, lambda t: 48 * (t // 2 + 1)))
                hold(sp, t_full, val(b, lambda t: NK * (t - 1) + NT * (g + 1) if t else 0))
                sp.dma_start(kst_c[:, HG * g:HG * g + HG, :], kst_n[:, HG * g:HG * g + HG, :]
                             ).then_inc(kst_c_in[g], 16)
                hold(sp, v3_ready, val(b, lambda t: 5 * (t // 2 + 1)))
                hold(sp, o_full, val(b, lambda t: 2 * NJ * (t - 1) + NJ * (g + 1) if t else 0))
                sp.dma_start(v_c[:, g, :], v_n[:, g, :]).then_inc(v_c_in[g], 16)

            def store(b):
                hold(sp, y_ready, val(b, lambda t: 2 * (t + 1)))
                sp.dma_start(out[bass.ds(b.row(), QB), :].rearrange("(j p) d -> p j d", p=P), y[:]
                             ).then_inc(y_out, 16)

            b0 = Blk(0, 0)
            sp.dma_start(wk[:], wkT.rearrange("(c p) n -> p c n", p=P)).then_inc(consts_in, 16)
            sp.dma_start(id32[:], ident).then_inc(consts_in, 16)
            sp.dma_start(wq[:], wqT.rearrange("(c p) n -> p c n", p=P)).then_inc(consts_in, 16)
            sp.dma_start(wv[:], wvT.rearrange("(c p) n -> p c n", p=P)).then_inc(consts_in, 16)
            sp.wait_ge(pool_cleared, 1)
            sp.dma_start(m8[:], mask.rearrange("(j p) k -> p j k", p=P)).then_inc(masks_in, 16)
            sp.dma_start(mt8[:], maskT[0:P, :]).then_inc(masks_in, 16)
            for q in range(4):
                sp.dma_start(mtt8[32 * q:32 * q + TAIL, :], maskT[P:SK, :]).then_inc(masks_in, 16)
            sp.wait_ge(dve_cleared, 3)
            stack_k(b0)
            q_to_dram(b0)
            for g in range(2):
                stack_q(b0, g)
            for g in range(2):
                keys_to_attend(b0, g)
            sp.dma_start(wo[:], woT.rearrange("(c p) n -> p c n", p=P)).then_inc(late_consts_in, 16)
            sp.dma_start(wdown[:], downT.rearrange("(c p) n -> p c n", p=P)).then_inc(late_consts_in, 16)
            sp.dma_start(wup[:], upT).then_inc(late_consts_in, 16)
            sp.dma_start(wrout[:], routerT.rearrange("(c p) n -> p c n", p=P)).then_inc(late_consts_in, 16)
            sp.dma_start(tri_sb[:], tri).then_inc(late_consts_in, 16)
            q_to_dram(b0.at(1))
            for g in range(2):
                stack_q(b0.at(1), g)

            def slot(sl):
                b = sl.b
                if sl.has_kv:
                    stack_k(b.at(2))
                if sl.has_project:
                    q_to_dram(sl.prj)
                    stack_q(sl.prj, 0)
                if b.par == 1 and sl.has_project:
                    keys_to_attend(b.at(1), 0)
                if sl.has_project:
                    stack_q(sl.prj, 1)
                if sl.has_finish:
                    store(sl.fin)
                if b.par == 1 and sl.has_project:
                    keys_to_attend(b.at(1), 1)

            run(sp, slot)
            store(Blk(NB, -1))
            sp.wait_ge(y_out, 16 * NBLK)

        @block.gpsimd
        def _(pool):
            def copy_tail(b, part=0):
                pool.wait_ge(ctx_in, val(b, lambda t: 16 * (t // 2 + 1)))
                hold(pool, d_full[1], val(b, lambda t: ordinal["v1", t - 2] if t >= 2 else 0))
                for c in range(KC):
                    ins = pool.tensor_copy(ctail[:, c, :, 0:TAIL],
                                           cin[:, c, P:SK].unsqueeze(1).broadcast_to([P, 4, TAIL]))
                ins.then_inc(tail_copied, 1)

            def residual(b, k):
                g, kk, _, _ = tile_of(k)
                pool.wait_ge(t_done, val(b, lambda t: NK * t + k + 1))
                wait(pool, o_full, val(b, lambda t: 2 * NJ * (t - 1) + NJ * (g + 1) if t else 0))
                pool.tensor_tensor(pb[g][:, kk, :], p32[:, k % NRING, :], pa[g][:, kk, :],
                                   ALU.subtract).then_inc(pb_pool, 1)

            def normalise(b, g, j):
                pool.wait_ge(o_free, val(b, lambda t: 2 * NJ * t + NJ * g + j + 1))
                if g == 0 and j == 0:
                    wait(pool, d_full[1], val(b, lambda t: ordinal["oT1", t - 1] if t else 0))
                pool.tensor_tensor(on[:, j, P * g:P * g + P].rearrange("p (h d) -> p h d", d=HD),
                                   osum[:, j % 2], rden[:, j % 2].unsqueeze(2).broadcast_to([P, HG, HD]),
                                   ALU.mult).then_inc(on_ready, 1)

            def normalise0(b, j):
                normalise(b, 0, j)

            def normalise1(b, j):
                normalise(b, 1, j)

            def add_norms(b, part=0):
                pool.wait_ge(x2_ready, val(b, lambda t: NJ * (t + 1)))
                wait(pool, y_ready, val(b, lambda t: 2 * t))
                pool.tensor_tensor(z[:], x1[:], x2[:], ALU.add).then_inc(z_ready, 1)

            pool.memset(mtt8[:], 0).then_inc(pool_cleared, 1)
            pool.memset(kp[:], 0.0).then_inc(pool_cleared, 1)
            pool.memset(ctail[:], 0.0).then_inc(ctail_cleared, 1)
            pool.wait_ge(ctail_cleared, 1)
            copy_tail(Blk(0, 0))

            def slot(sl):
                do = {"pb": residual, "o_norm0": normalise0, "o_norm1": normalise1, "tail": copy_tail,
                      "z": add_norms}
                for name, b, part in sl.stages(POOL_AT):
                    do[name](b, part)

            run(pool, slot)
            for j in range(NJ):
                normalise(Blk(NB, -1), 1, j)
            add_norms(Blk(NB, -1))

        @block.scalar
        def _(act):
            def load_ctx(b):
                wait(act, d_full[1], val(b, lambda t: ordinal["v1", t - 2] if t >= 2 else 0))
                wait(act, tail_copied, val(b, lambda t: t // 2))
                bi = b.i + b.o // 2
                src = ctxT[bi:bi + 1] if isinstance(bi, int) else ctxT[bass.ds(bi, 1)]
                act.dma_start(cin[:], src.rearrange("a (c p) k -> p (a c) k", p=P)).then_inc(ctx_in, 16)

            def load_x(b):
                wait(act, xn_ready, val(b, lambda t: NJ * (t - 1)))
                act.dma_start(xin[b.par][:], x[bass.ds(b.row(), QB), :].rearrange("(j p) d -> p j d", p=P)
                             ).then_inc(x_in[b.par], 16)

            def load_xres(b):
                wait(act, x1_ready, val(b, lambda t: 2 * (t - 1)))
                act.dma_start(xres[b.par][:], x[bass.ds(b.row(), QB), :].rearrange("(j p) d -> p j d", p=P)
                             ).then_inc(xres_in[b.par], 16)

            def exps(b, k):
                g, kk, _, _ = tile_of(k)
                act.wait_ge(t_full, val(b, lambda t: NK * t + k + 1))
                engine_has = (k - NRING) % NK in POOL_AT["pb"]
                wait(act, pb_pool if engine_has else pb_dve,
                     val(b, lambda t: pb_count(NK * t + k - NRING + 1, engine_has) if NK * t + k >= NRING else 0))
                act.activation(p32[:, k % NRING, :], ps_t[k % 2][:], ACT.Exp)
                if kk == 0:
                    wait(act, o_full, val(b, lambda t: 2 * NJ * (t - 1) + NJ * (g + 1) if t else 0))
                act.activation(pa[g][:, kk, :], ps_t[k % 2][:], ACT.Exp).then_inc(t_done, 1)

            def norm1(b, j):
                act.wait_ge(ln1_scale, val(b, lambda t: t + 1))
                wait(act, d_full[1], val(b, lambda t: ordinal["xT1", t - 1] if t else 0))
                act.activation(xn[:, j, :], xin[b.par][:, j, :], ACT.Identity, bias=nmr[:, j:j + 1],
                               scale=rstd[:, j:j + 1]).then_inc(xn_ready, 1)

            def norm2(b, j):
                act.wait_ge(ln2_scale, val(b, lambda t: t + 1))
                wait(act, d_full[1], val(b, lambda t: ordinal["nT1", t - 1] if t else 0))
                wait(act, z_ready, val(b, lambda t: t))
                act.activation(x2[:, j, :], x1[:, j, :], ACT.Identity, bias=nmr2[:, j:j + 1],
                               scale=rstd2[:, j:j + 1]).then_inc(x2_ready, 1)

            def xT(b, c):
                src = full(act, b, f"xT{c}")
                wait(act, d_full[1], val(b, lambda t: ordinal["q1", t - 1] if t else 0))
                act.copy(xnT[:, c, :], src[:]).then_inc(d_free[c], 1)

            def q1(b, m):
                src = full(act, b, f"q{m}")
                wait(act, q_dram, val(b, lambda t: 48 * t))
                act.activation(qp[:, 0, m, :], src[:], ACT.Copy, scale=SCALE).then_inc(q1_ready, 1)

            def q2(b, m):
                act.wait_ge(qr_ready, val(b, lambda t: 2 * t + m + 1))
                act.copy(qp[:, 1, m, :], qr[:, m, :]).then_inc(q2_ready, 1)

            def k1(b, m):
                src = full(act, b, f"k{m}")
                wait(act, k_dram, val(b, lambda t: 48 * (t // 2)))
                if isinstance(b.i, int) and b.i == 0 and b.o == 0:
                    act.wait_ge(pool_cleared, 2)
                act.copy(kp[:, 0, m, 0:SK], src[:, 0:SK]).then_inc(k1_ready, 1)

            def k2(b, m):
                act.wait_ge(kr_ready, val(b, lambda t: 2 * (t // 2) + m + 1))
                act.copy(kp[:, 1, m, 0:SK], kr[:, m, :]).then_inc(k2_ready, 1)

            def v_main(part):
                v = v_n[:].rearrange("p g (h e) -> p g h e", e=VW)
                return v[:, :, 0:HG, 1 + HD * part:1 + HD * part + HD]

            def v1(b, tail):
                src = full(act, b, f"v{tail}")
                for g in range(2):
                    wait(act, v_c_in[g], val(b, lambda t: 16 * (t // 2)))
                if isinstance(b.i, int) and b.i == 0 and b.o == 0:
                    act.wait_ge(dve_cleared, 2)
                if tail:
                    for q in range(4):
                        rows = slice(32 * q, 32 * q + 32)
                        ins = act.copy(v_tail(q, 0), vt_in(src[rows, 0:D], q))
                else:
                    for g in range(2):
                        ins = act.copy(v_main(0)[:, g], src[:, P * g:P * g + P].rearrange("p (h d) -> p h d", d=HD))
                ins.then_inc(v1_ready, 1)

            def vt_in(a, q):
                return a.rearrange("p (gg h d) -> p gg h d", gg=4, d=HD)[:, :, q, :]

            def v_tail(q, part):
                v = v_n[32 * q:32 * q + 32].rearrange("p g (a gg h e) -> p g a gg h e", a=2, gg=2, e=VW)
                return v[:, :, 1, :, q, 1 + HD * part:1 + HD * part + HD]

            def v2(b, tail):
                act.wait_ge(vr_ready, val(b, lambda t: 2 * (t // 2) + tail + 1))
                if tail:
                    for q in range(4):
                        ins = act.copy(v_tail(q, 1), vt_in(vr[32 * q:32 * q + 32, 1, :], q))
                else:
                    for g in range(2):
                        ins = act.copy(v_main(1)[:, g], vr[:, 0, P * g:P * g + P].rearrange("p (h d) -> p h d", d=HD))
                ins.then_inc(v2_ready, 1)

            def max_rows(b, g):
                name = f"max{g}"
                src = full(act, b, name)
                wait(act, nm_rows[(b.par + 1) % 2][g], val(b, lambda t: 16 * ((t - 1) // 2 + 1) if t else 0))
                act.copy(nmT[g][:], src[0:3 * HG, 0:QB // 2].bitcast(BF16)).then_inc(d_free[bank_of[name]], 1)
                act.wait_ge(d_free[bank_of[name]], nth(b, name))
                act.dma_start(qst[b.par][NROW:NMAX, HG * g:HG * g + HG, :], nmT[g][:]).then_inc(nm_rows[b.par][g], 16)

            def by_chunk(bank):
                return bank[:].rearrange("p (c n) -> p c n", c=KC)

            def oT_out(b, p):
                src = full(act, b, f"oT{p}")
                wait(act, d_full[1], val(b, lambda t: ordinal["wo1", t - 1] if t else 0))
                act.copy(oT[:, :, 2 * P * p:2 * P * (p + 1)], by_chunk(src)).then_inc(d_free[p], 1)

            def nT_out(b, p):
                src = full(act, b, f"nT{p}")
                wait(act, d_full[1], val(b, lambda t: ordinal["down1", t - 1] if t else 0))
                act.copy(x2T[:, :, 2 * P * p:2 * P * (p + 1)], by_chunk(src)).then_inc(d_free[p], 1)

            def gate_exp(b, part=0):
                act.wait_ge(g_diff, val(b, lambda t: t // 2 + 1))
                act.activation(g_sel[:, 2, :], g_sel[:, 1, :], ACT.Exp).then_inc(g_exp, 1)

            def dn_out(b, p):
                src = full(act, b, f"down{p}")
                act.wait_ge(g_col_ready, val(b, lambda t: t // 2 + 1))
                wait(act, d_full[1], val(b, lambda t: ordinal["up1", t - 1] if t else 0))
                act.activation(dn[:, 2 * P * p:2 * P * (p + 1)], src[:, 0:2 * P], ACT.Copy, scale=g_col[:, 0:1]
                               ).then_inc(d_free[p], 1)

            DO = {"exp": exps, "k1": k1, "k2": k2, "v1": v1, "v2": v2, "norm1_x": norm1, "xT": xT, "q1": q1, "q2": q2,
                  "oT": oT_out, "norm2_x": norm2, "nT": nT_out, "gexp": gate_exp, "down": dn_out, "max": max_rows}

            b0 = Blk(0, 0)
            load_x(b0)
            load_ctx(b0)
            load_x(b0.at(1))
            for name, b, part in listed(ACT_FIRST, ACT_AT, FIRST):
                DO[name](b, part)

            def slot(sl):
                if sl.has_project and sl.b.par == 0:
                    load_x(sl.b.at(2))
                    load_x(sl.b.at(3))
                if sl.has_kv:
                    load_ctx(sl.b.at(2))
                load_xres(sl.b)
                for name, b, part in sl.stages(ACT_AT):
                    DO[name](b, part)

            run(act, slot)
            for name, b, part in listed(ACT_LAST, ACT_AT, LAST):
                DO[name](b, part)

        @block.vector
        def _(dve):
            STEPS = {"ln1b": 1, "ln2b": 1, "max": 1, "gate_a": 8, "gate_b": 3, "ln1a": 1, "ln2a": 1}
            order = [(name, b.o, part) for name, b, part in listed(DVE_FIRST, DVE_AT, FIRST) if name in STEPS]
            for sl in slots():
                order += [(name, 2 * b.i + b.o, part) for name, b, part in sl.stages(DVE_AT) if name in STEPS]
            order += [(name, NBLK - 1, part) for name, _, part in listed(DVE_LAST, DVE_AT, LAST) if name in STEPS]
            done, total = {}, 0
            for name, t, part in order:
                done[f"{name}{part}", t] = total
                ends = {"ln1b": (LN_STEPS - 1,), "ln2b": (LN_STEPS - 1,), "max": (MAX_STEPS - 1, 2 * MAX_STEPS - 1)}
                total += 0 if part in ends.get(name, ()) else STEPS[name]

            def step(ins, b, name, n):
                ins.then_inc(dve_step, 1)
                if name.startswith("ln"):
                    hold(dve, dve_step, val(b, lambda t: done[name, t] + n))
                else:
                    dve.wait_ge(dve_step, val(b, lambda t: done[name, t] + n))

            def mark(ins):
                ins.then_inc(dve_step, 1)

            def scales(b, name, n, free, stats, mv, var, tmp, rstd, nmr, ready):
                if n == 0:
                    hold(dve, free, val(b, lambda t: NJ * t))
                    hold(dve, dve_step, val(b, lambda t: done[f"{name}0", t]))
                    for j in range(NJ):
                        ins = dve.bn_aggr(mv[:, j, :], stats[:, j, :])
                    mark(ins)
                    return
                dve.wait_ge(dve_step, val(b, lambda t: done[f"{name}{n - 1}", t] + 1))
                if n == 1:
                    ins = dve.tensor_scalar(var[:], mv[:, :, 1], EPS, None, ALU.add)
                elif n == 2:
                    ins = dve.tensor_single_scalar(rstd[:].bitcast(I32), var[:].bitcast(I32), 1,
                                                   ALU.logical_shift_right)
                elif n == 3:
                    ins = dve.tensor_scalar(rstd[:].bitcast(I32), rstd[:].bitcast(I32), -1.0, RSQRT_BITS,
                                            ALU.mult, ALU.add)
                elif n == LN_STEPS - 1:
                    dve.scalar_tensor_tensor(nmr[:], mv[:, :, 0], -1.0, rstd[:], ALU.mult, ALU.mult
                                             ).then_inc(ready, 1)
                    return
                elif n % 3 == 1:
                    ins = dve.tensor_tensor(tmp[:], rstd[:], rstd[:], ALU.mult)
                elif n % 3 == 2:
                    ins = dve.scalar_tensor_tensor(tmp[:], tmp[:], -0.5, var[:], ALU.mult, ALU.mult)
                else:
                    ins = dve.scalar_tensor_tensor(rstd[:], tmp[:], 1.5, rstd[:], ALU.add, ALU.mult)
                mark(ins)

            def ln1a(b, j):
                dve.wait_ge(x_in[b.par], val(b, lambda t: 16 * (t // 2 + 1)))
                mark(dve.bn_stats(stats[:, j, :], xin[b.par][:, j, :]))

            def ln1b(b, n):
                scales(b, "ln1b", n, xn_ready, stats, mv, var, newt, rstd, nmr, ln1_scale)

            def ln2a(b, j):
                dve.wait_ge(x1_ready, val(b, lambda t: 2 * t + j // 2 + 1))
                mark(dve.bn_stats(stats2[:, j, :], x1[:, j, :]))

            def ln2b(b, n):
                scales(b, "ln2b", n, x2_ready, stats2, mv2, var2, newt2, rstd2, nmr2, ln2_scale)

            def q_rest(b, m):
                dve.wait_ge(q1_ready, val(b, lambda t: 2 * t + m + 1))
                wait(dve, q3_ready, val(b, lambda t: 2 * t))
                wait(dve, q2_ready, val(b, lambda t: 2 * t))
                dve.scalar_tensor_tensor(qr[:, m, :], ps_d[m][:], SCALE, qp[:, 0, m, :], ALU.mult,
                                         ALU.subtract).then_inc(qr_ready, 1)
                dve.wait_ge(qr_ready, val(b, lambda t: 2 * t + m + 1))
                dve.sem_inc(d_free[m], 1)

            def q3(b, m):
                dve.wait_ge(q2_ready, val(b, lambda t: 2 * t + m + 1))
                dve.tensor_tensor(qp[:, 2, m, :], qr[:, m, :], qp[:, 1, m, :], ALU.subtract).then_inc(q3_ready, 1)

            def k_rest(b, m):
                dve.wait_ge(k1_ready, val(b, lambda t: 2 * (t // 2) + m + 1))
                wait(dve, k3_ready, val(b, lambda t: 2 * (t // 2)))
                dve.tensor_tensor(kr[:, m, :], ps_d[m][:, 0:SK], kp[:, 0, m, 0:SK], ALU.subtract
                                  ).then_inc(kr_ready, 1)
                dve.wait_ge(kr_ready, val(b, lambda t: 2 * (t // 2) + m + 1))
                dve.sem_inc(d_free[m], 1)

            def k3(b, m):
                dve.wait_ge(k2_ready, val(b, lambda t: 2 * (t // 2) + m + 1))
                dve.tensor_tensor(kp[:, 2, m, 0:SK], kr[:, m, :], kp[:, 1, m, 0:SK], ALU.subtract
                                  ).then_inc(k3_ready, 1)

            def heads(a):
                return a.rearrange("p (h d) -> p h d", d=HD)

            def v_main(g, part):
                return v_n[:, g, 0:HG * VW].rearrange("p (h e) -> p h e", e=VW)[:, :, 1 + HD * part:1 + HD * part + HD]

            def v_tail(q, part):
                v = v_n[32 * q:32 * q + 32].rearrange("p g (a gg h e) -> p g a gg h e", a=2, gg=2, e=VW)
                return v[:, :, 1, :, q, 1 + HD * part:1 + HD * part + HD]

            def vt_in(a, q):
                return a.rearrange("p (g gg h d) -> p g gg h d", g=2, gg=2, d=HD)[:, :, :, q, :]

            def v_rest(b, tail):
                dve.wait_ge(v1_ready, val(b, lambda t: 2 * (t // 2) + tail + 1))
                wait(dve, v3_ready, val(b, lambda t: 5 * (t // 2)))
                if tail:
                    for q in range(4):
                        r = slice(32 * q, 32 * q + 32)
                        ins = dve.tensor_tensor(vt_in(vr[r, 1, :], q), vt_in(ps_d[1][r, 0:D], q), v_tail(q, 0),
                                                ALU.subtract)
                else:
                    for g in range(2):
                        ins = dve.tensor_tensor(heads(vr[:, 0, P * g:P * g + P]), heads(ps_d[0][:, P * g:P * g + P]),
                                                v_main(g, 0), ALU.subtract)
                ins.then_inc(vr_ready, 1)
                dve.wait_ge(vr_ready, val(b, lambda t: 2 * (t // 2) + tail + 1))
                dve.sem_inc(d_free[tail], 1)

            def v3(b, tail):
                dve.wait_ge(v2_ready, val(b, lambda t: 2 * (t // 2) + tail + 1))
                if tail:
                    for q in range(4):
                        dve.tensor_tensor(v_tail(q, 2), vt_in(vr[32 * q:32 * q + 32, 1, :], q), v_tail(q, 1),
                                          ALU.subtract).then_inc(v3_ready, 1)
                    return
                for g in range(2):
                    ins = dve.tensor_tensor(v_main(g, 2), heads(vr[:, 0, P * g:P * g + P]), v_main(g, 1),
                                            ALU.subtract)
                ins.then_inc(v3_ready, 1)

            def maxima(b, u):
                kb, j = UNITS[u]
                h0 = HPB * kb
                n = min(HPB, H - h0)
                if isinstance(b.i, int) and b.i == 0 and b.o == 0 and u == 0:
                    dve.wait_ge(masks_ready, 1)
                if u in MASKED_BY_PE:
                    dve.wait_ge(s_full, val(b, lambda t: len(UNITS) * t + u + 1))
                    dve.tensor_reduce(smax[:, j, h0:h0 + n],
                                      ps_s[u % 2][:, 0:n * SK].rearrange("p (h k) -> p h k", k=SK),
                                      X, ALU.max).then_inc(s_free, 1)
                    return
                hold(dve, s_full, val(b, lambda t: len(UNITS) * t + u + 1))
                for h in range(n):
                    ins = dve.tensor_tensor_reduce(masked[:, u % 2, h], ps_s[u % 2][:, h * SK:(h + 1) * SK],
                                                   maskq[:, NJ * b.par + j, :], 1.0, LOWEST, ALU.add, ALU.max,
                                                   accum_out=smax[:, j, h0 + h:h0 + h + 1])
                ins.then_inc(s_free, 1)

            def max_parts(b, part):
                g, n = divmod(part, MAX_STEPS)
                hs = slice(HG * g, HG * g + HG)
                if n == 0:
                    dve.wait_ge(s_free, val(b, lambda t: len(UNITS) * t + (len(UNITS) if g else 3 * NJ)))
                    k = bank_of[f"max{g}"]
                    wait(dve, d_full[k], val(b, lambda t: ordinal[f"max{g}", t - 1] if t else 0))
                    mark(dve.tensor_scalar(nms[:], smax[:, :, hs], -1.0, SHIFT, ALU.mult, ALU.add))
                    return
                dve.wait_ge(dve_step, val(b, lambda t: done[f"max{part - 1}", t] + 1))
                if n == 1:
                    mark(dve.tensor_copy(nmp[g][:, :, 0, :], nms[:]))
                elif n == 2:
                    mark(dve.tensor_tensor(nmr1[:], nms[:], nmp[g][:, :, 0, :], ALU.subtract))
                elif n == 3:
                    mark(dve.tensor_copy(nmp[g][:, :, 1, :], nmr1[:]))
                else:
                    dve.tensor_tensor(nmp[g][:, :, 2, :], nmr1[:], nmp[g][:, :, 1, :], ALU.subtract
                                      ).then_inc(nmp_ready[g], 1)

            first_pb = [min(k for k in DVE_AT["pb"] if k // NT == g) for g in range(2)]

            def residual(b, k):
                g, kk, _, _ = tile_of(k)
                dve.wait_ge(t_done, val(b, lambda t: NK * t + k + 1))
                if k in first_pb:
                    wait(dve, o_full, val(b, lambda t: 2 * NJ * (t - 1) + NJ * (g + 1) if t else 0))
                dve.tensor_tensor(pb[g][:, kk, :], p32[:, k % NRING, :], pa[g][:, kk, :], ALU.subtract
                                  ).then_inc(pb_dve, 1)

            def sum_o(b, g, j):
                dve.wait_ge(o_full, val(b, lambda t: 2 * NJ * t + NJ * g + j + 1))
                wait(dve, on_ready, val(b, lambda t: max(0, 2 * NJ * t + NJ * g + j - 1)))
                o = ps_o[j % 2][:, 0:HG * VW].rearrange("p (h e) -> p h e", e=VW)
                dve.tensor_reduce(osum[:, j % 2], o[:, :, 1:VW].rearrange("p h (x d) -> p h d x", x=3),
                                  X, ALU.add)
                dve.reciprocal(rden[:, j % 2], o[:, :, 0]).then_inc(o_free, 1)

            def add_x(b, p):
                dve.wait_ge(xres_in[b.par], val(b, lambda t: 16 * (t // 2 + 1)))
                wait(dve, z_ready, val(b, lambda t: t))
                src = full(dve, b, f"wo{p}")
                dve.tensor_tensor(x1[:, 2 * p:2 * p + 2, :], xres[b.par][:, 2 * p:2 * p + 2, :],
                                  src[:].rearrange("p (j d) -> p j d", j=2), ALU.add).then_inc(x1_ready, 1)
                dve.wait_ge(x1_ready, val(b, lambda t: 2 * t + p + 1))
                dve.sem_inc(d_free[p], 1)

            def gate_a(b, part=0):
                src = full(dve, b, "logit0")
                g = "gate_a0"
                dve.wait_ge(late_consts_in, 80)
                step(dve.tensor_copy(g_l[:], src[0:1, 0:E]), b, g, 1)
                dve.sem_inc(d_free[0], 1)
                l_j = g_l[:].unsqueeze(1).broadcast_to([1, E, E])
                l_e = g_l[:].unsqueeze(2).broadcast_to([1, E, E])
                mark(dve.tensor_tensor(g_eq[:], l_j, l_e, ALU.is_equal))
                mark(dve.tensor_tensor(g_gt[:], l_j, l_e, ALU.is_gt))
                step(dve.tensor_reduce(g_s[:, 0:1], g_l[:], X, ALU.max), b, g, 4)
                step(dve.tensor_tensor(g_eq[:], g_eq[:], tri_sb[:].rearrange("a (e j) -> a e j", j=E), ALU.mult),
                     b, g, 5)
                step(dve.tensor_tensor(g_gt[:], g_gt[:], g_eq[:], ALU.add), b, g, 6)
                step(dve.tensor_reduce(g_sel[:, 3, :], g_gt[:], X, ALU.add), b, g, 7)
                step(dve.tensor_single_scalar(g_sel[:, 0, :], g_sel[:, 3, :], 2.0, ALU.is_lt), b, g, 8)
                dve.tensor_scalar(g_sel[:, 1, :], g_l[:], g_s[:, 0:1], None, ALU.subtract).then_inc(g_diff, 1)

            def gate_b(b, part=0):
                g = "gate_b0"
                dve.wait_ge(g_exp, val(b, lambda t: t // 2 + 1))
                step(dve.tensor_tensor(g_sel[:, 4, :], g_sel[:, 2, :], g_sel[:, 0, :], ALU.mult), b, g, 1)
                step(dve.tensor_reduce(g_s[:, 1:2], g_sel[:, 4, :], X, ALU.add), b, g, 2)
                step(dve.reciprocal(g_s[:, 2:3], g_s[:, 1:2]), b, g, 3)
                dve.tensor_scalar(g_row[:], g_sel[:, 4, :].unsqueeze(2).broadcast_to([1, E, R]), g_s[:, 2:3], None,
                                  ALU.mult).then_inc(g_row_ready, 1)

            def gate_col(b, part=0):
                src = full(dve, b, "gcol0")
                wait(dve, d_free[1], val(b, lambda t: ordinal["down1", t - 1] if t else 0))
                dve.tensor_copy(g_col[:], src[:, 0:1]).then_inc(g_col_ready, 1)
                dve.wait_ge(g_col_ready, val(b, lambda t: t // 2 + 1))
                dve.sem_inc(d_free[1], 1)

            def add_z(b, p):
                dve.wait_ge(z_ready, val(b, lambda t: t + 1))
                wait(dve, y_out, val(b, lambda t: 16 * t))
                name = f"up{p}"
                src = full(dve, b, name)
                dve.tensor_tensor(y[:, 2 * p:2 * p + 2, :], z[:, 2 * p:2 * p + 2, :],
                                  src[:].rearrange("p (j d) -> p j d", j=2), ALU.add).then_inc(y_ready, 1)
                dve.wait_ge(y_ready, val(b, lambda t: 2 * t + p + 1))
                dve.sem_inc(d_free[bank_of[name]], 1)

            def sum0(b, j):
                sum_o(b, 0, j)

            def sum1(b, j):
                sum_o(b, 1, j)

            def open_masks(b, part):
                dve.wait_ge(masks_in, 96)
                for dst, src in ((maskq, m8), (maskk, mt8), (maskt, mtt8)):
                    dve.tensor_scalar(dst[:], src[:], -MASKED, MASKED, ALU.mult, ALU.add).then_inc(masks_ready, 1)

            def identity(b, part):
                dve.wait_ge(consts_in, 64)
                dve.tensor_copy(id16[:], id32[:]).then_inc(id16_ready, 1)

            DO = {"id16": identity, "masks": open_masks, "pb": residual, "sum0": sum0, "sum1": sum1, "unit": maxima,
                  "max": max_parts, "kr": k_rest, "k3": k3,
                  "vr": v_rest, "v3": v3, "ln1a": ln1a, "ln1b": ln1b, "addx": add_x, "ln2a": ln2a, "ln2b": ln2b,
                  "qr": q_rest, "q3": q3, "gate_a": gate_a, "gate_b": gate_b, "gcol": gate_col, "y": add_z}

            b0 = Blk(0, 0)
            dve.memset(v_n[:], 0.0).then_inc(v_zero, 1)
            dve.wait_ge(v_zero, 1)
            dve.memset(v_n[:, :, 0:HG * VW].rearrange("p g (h e) -> p g h e", e=VW)[:, :, :, 0], 1.0
                       ).then_inc(dve_cleared, 1)
            for q in range(4):
                v = v_n[32 * q:32 * q + TAIL].rearrange("p g (a gg h e) -> p g a gg h e", a=2, gg=2, e=VW)
                ins = dve.memset(v[:, :, 1, :, q, 0], 1.0)
            ins.then_inc(dve_cleared, 1)
            dve.memset(kst_n[NROW:NMAX], 1.0).then_inc(dve_cleared, 1)
            dve.memset(one1[:], 1.0).then_inc(one_ready, 1)
            for name, b, part in listed(DVE_FIRST, DVE_AT, FIRST):
                DO[name](b, part)

            def slot(sl):
                for name, b, part in sl.stages(DVE_AT):
                    DO[name](b, part)

            run(dve, slot)
            for name, b, part in listed(DVE_LAST, DVE_AT, LAST):
                DO[name](b, part)

        @block.tensor
        def _(pe):
            def project_k(b, m):
                pe.wait_ge(ctx_in, val(b, lambda t: 16 * (t // 2 + 1)))
                dst = fill(pe, b, f"k{m}")
                for c in range(KC):
                    mm = pe.matmul(dst[:, 0:SK], wk[:, c, P * m:P * m + P], cin[:, c, :],
                                   start=c == 0, stop=c == KC - 1)
                mm.then_inc(d_full[m], 1)

            def project_v(b, tail):
                if tail:
                    pe.wait_ge(tail_copied, val(b, lambda t: t // 2 + 1))
                else:
                    pe.wait_ge(ctx_in, val(b, lambda t: 16 * (t // 2 + 1)))
                dst = fill(pe, b, f"v{tail}")
                for c in range(KC):
                    keys = ctail[:, c].rearrange("p q k -> p (q k)") if tail else cin[:, c, 0:P]
                    mm = pe.matmul(dst[:, 0:D], keys, wv[:, c, :], start=c == 0, stop=c == KC - 1)
                mm.then_inc(d_full[tail], 1)

            def turn_pair(b, name, src, p):
                dst = fill(pe, b, f"{name}{p}")
                for c in range(KC):
                    for j in range(2):
                        mm = pe.transpose(dst[:, P * (2 * c + j):P * (2 * c + j + 1)],
                                          src[:, 2 * p + j, P * c:P * c + P], id32[:])
                mm.then_inc(d_full[p], 1)

            def turn_x(b, c):
                pe.wait_ge(xn_ready, val(b, lambda t: NJ * (t + 1)))
                dst = fill(pe, b, f"xT{c}")
                for j in range(NJ):
                    mm = pe.transpose(dst[:, P * j:P * j + P], xn[:, j, P * c:P * c + P], id32[:])
                mm.then_inc(d_full[c], 1)

            def turn_o(b, p):
                pe.wait_ge(on_ready, val(b, lambda t: 2 * NJ * t + NJ + 2 * p + 2))
                turn_pair(b, "oT", on, p)

            def turn_n(b, p):
                pe.wait_ge(x2_ready, val(b, lambda t: NJ * t + 2 * p + 2))
                turn_pair(b, "nT", x2, p)

            def project_q(b, m):
                for c in range(KC):
                    pe.wait_ge(d_free[c], nth(b, f"xT{c}"))
                dst = fill(pe, b, f"q{m}")
                for c in range(KC):
                    mm = pe.matmul(dst[:], wq[:, c, P * m:P * m + P], xnT[:, c, :], start=c == 0,
                                   stop=c == KC - 1)
                mm.then_inc(d_full[m], 1)

            def score_unit(b, u):
                kb, j = UNITS[u]
                h0 = HPB * kb
                n = min(HPB, H - h0)
                keys = kst_c if b.par else kst_n
                if isinstance(b.i, int) and b.i == 0 and b.o == 0 and u == min(MASKED_BY_PE, default=None):
                    pe.wait_ge(id16_ready, 1)
                    pe.wait_ge(masks_ready, 1)
                if u == 0:
                    if b.par == 0:
                        pe.wait_ge(kst_n_in, val(b, lambda t: 48 * (t // 2 + 1)))
                    pe.wait_ge(q_stack[b.par][0], val(b, lambda t: 48 * (t // 2 + 1)))
                if b.par and kb in (0, 2) and j == 0:
                    pe.wait_ge(kst_c_in[kb // 2], val(b, lambda t: 16 * (t // 2 + 1)))
                if kb == 2 and j == 0:
                    pe.wait_ge(q_stack[b.par][1], val(b, lambda t: 48 * (t // 2 + 1)))
                wait(pe, s_free, val(b, lambda t: max(0, len(UNITS) * t + u - 1)))
                dst = ps_s[u % 2]
                if u in MASKED_BY_PE:
                    pe.matmul(dst[:, 0:n * SK].rearrange("p (h k) -> p h k", k=SK), id16[:],
                              maskq[:, NJ * b.par + j, :].unsqueeze(1).broadcast_to([P, n, SK]),
                              start=True, stop=False, skip_group_check=True)
                for h in range(n):
                    mm = pe.matmul(dst[:, h * SK:(h + 1) * SK], qst[b.par][0:NROW, h0 + h, P * j:P * j + P],
                                   keys[0:NROW, h0 + h, 0:SK], start=h == 0 and u not in MASKED_BY_PE,
                                   stop=h == n - 1,
                                   skip_group_check=True)
                mm.then_inc(s_full, 1)

            def score_tile(b, k):
                g, kk, gg, hq = tile_of(k)
                if kk == 0:
                    pe.wait_ge(nm_rows[b.par][g], val(b, lambda t: 16 * (t // 2 + 1)))
                    pe.wait_ge(kst_c_in[g], val(b, lambda t: 16 * (t // 2 + 1)))
                wait(pe, t_done, val(b, lambda t: max(0, NK * t + k - 1)))
                dst = ps_t[k % 2]
                h0 = HG * g + 4 * gg
                cols = slice(QB * b.par, QB * b.par + QB)
                if hq < 4:
                    pe.matmul(dst[:], kst_c[:, h0 + hq, 0:P], qst[b.par][:, h0 + hq, :], start=True, stop=False)
                    pe.matmul(dst[:], id16[:], maskk[:, cols], start=False, stop=True).then_inc(t_full, 1)
                    return
                for q in range(4):
                    pe.matmul(dst[32 * q:32 * q + 32, :], kst_c[:, h0 + q, P:SKP], qst[b.par][:, h0 + q, :],
                              start=True, stop=False, skip_group_check=True)
                pe.matmul(dst[:], id16[:], maskt[:, cols], start=False, stop=True,
                          skip_group_check=True).then_inc(t_full, 1)

            def pv(b, g, j):
                if j == 0:
                    pe.wait_ge(pb_dve, val(b, lambda t: pb_count(NK * t + NT * (g + 1), False)))
                    pe.wait_ge(pb_pool, val(b, lambda t: pb_count(NK * t + NT * (g + 1), True)))
                    pe.wait_ge(v_c_in[g], val(b, lambda t: 16 * (t // 2 + 1)))
                wait(pe, o_free, val(b, lambda t: max(0, 2 * NJ * t + NJ * g + j - 1)))
                dst = ps_o[j % 2]
                first = True
                o = dst[:, 0:HG * VW].rearrange("p (h e) -> p h e", e=VW)
                v = v_c[:, g].rearrange("p (h e) -> p h e", e=VW)
                for part, w in ((pa[g], VW), (pb[g], VWB)):
                    for kk in range(NT):
                        gg, hq = divmod(kk, 5)
                        h, n = (4 * gg + hq, 1) if hq < 4 else (4 * gg, 4)
                        hv = h if hq < 4 else HG + h
                        mm = pe.matmul(o[:, h:h + n, 0:w], part[:, kk, P * j:P * j + P], v[:, hv:hv + n, 0:w],
                                       start=first, stop=w == VWB and kk == NT - 1, skip_group_check=True)
                        first = False
                mm.then_inc(o_full, 1)

            def pv0(b, j):
                pv(b, 0, j)

            def pv1(b, j):
                pv(b, 1, j)

            def apply_wo(b, p):
                pe.wait_ge(d_free[p], nth(b, f"oT{p}"))
                pe.wait_ge(late_consts_in, 80)
                dst = fill(pe, b, f"wo{p}")
                for j in range(2):
                    for c in range(KC):
                        mm = pe.matmul(dst[:, D * j:D * j + D], oT[:, c, P * (2 * p + j):P * (2 * p + j) + P],
                                       wo[:, c, :], start=c == 0, stop=c == KC - 1, skip_group_check=True)
                mm.then_inc(d_full[p], 1)

            def logits(b, part=0):
                pe.wait_ge(d_free[0], nth(b, "nT0"))
                dst = fill(pe, b, "logit0")
                for c in range(KC):
                    mm = pe.matmul(dst[0:1, 0:E], x2T[:, c, 0:1], wrout[:, c, :], start=c == 0, stop=c == KC - 1)
                mm.then_inc(d_full[0], 1)

            def gate_col(b, part=0):
                pe.wait_ge(one_ready, 1)
                pe.wait_ge(g_row_ready, val(b, lambda t: t // 2 + 1))
                dst = fill(pe, b, "gcol0")
                pe.matmul(dst[:, 0:1], g_row[:].rearrange("a e r -> a (e r)"), one1[:], start=True, stop=True
                          ).then_inc(d_full[1], 1)

            def down(b, p):
                pe.wait_ge(d_free[p], nth(b, f"nT{p}"))
                dst = fill(pe, b, f"down{p}")
                for c in range(KC):
                    mm = pe.matmul(dst[:, 0:2 * P], wdown[:, c, :], x2T[:, c, 2 * P * p:2 * P * (p + 1)],
                                   start=c == 0, stop=c == KC - 1)
                mm.then_inc(d_full[p], 1)

            def up(b, p):
                pe.wait_ge(d_free[p], nth(b, f"down{p}"))
                dst = fill(pe, b, f"up{p}")
                for j in range(2):
                    mm = pe.matmul(dst[:, D * j:D * j + D], dn[:, P * (2 * p + j):P * (2 * p + j) + P], wup[:],
                                   start=True, stop=True, skip_group_check=True)
                mm.then_inc(d_full[p], 1)

            def max_turn(b, g):
                dst = fill(pe, b, f"max{g}")
                hold(pe, nmp_ready[g], val(b, lambda t: t + 1))
                for j in range(NJ):
                    mm = pe.transpose(dst[0:3 * HG, 64 * j:64 * j + 64].bitcast(BF16),
                                      nmp[g][:, j].rearrange("p a h -> p (a h)"), id16[:])
                mm.then_inc(d_full[bank_of[f"max{g}"]], 1)

            DO = {"tile": score_tile, "pv0": pv0, "pv1": pv1, "unit": score_unit, "k": project_k, "v": project_v,
                  "oT": turn_o, "wo": apply_wo, "xT": turn_x, "q": project_q, "nT": turn_n, "logit": logits,
                  "gcol": gate_col, "down": down, "up": up, "max": max_turn}

            pe.wait_ge(consts_in, 64)
            for name, b, part in listed(PE_FIRST, PE_AT, FIRST):
                if name == "max" and part == 0:
                    pe.wait_ge(id16_ready, 1)
                    pe.wait_ge(masks_ready, 3)
                DO[name](b, part)

            def slot(sl):
                for name, b, part in sl.stages(PE_AT):
                    DO[name](b, part)

            run(pe, slot)
            for name, b, part in listed(PE_LAST, PE_AT, LAST):
                DO[name](b, part)


def kernel(x, ctx_1024, mask_1x1xSxS2_bk0, L0_xattn_W_q, L0_xattn_W_k, L0_xattn_W_v, L0_xattn_W_o,
           L0_ffn_router_w, L0_ffn_lora_down, L0_ffn_lora_up):
    import numpy as np
    import concourse.bacc as bacc
    from concourse.bass_utils import run_bass_kernel_spmd

    def laid(a):
        return np.ascontiguousarray(a)

    def by_pairs(w):
        return laid(np.asarray(w).T.reshape(D, H // 2, 2, HD).transpose(0, 2, 1, 3).reshape(D, D))

    mask2 = np.asarray(mask_1x1xSxS2_bk0).reshape(S, SK)
    arrays = {
        "x": laid(np.asarray(x).reshape(NB * S, D)),
        "ctxT": laid(np.asarray(ctx_1024).transpose(0, 2, 1)),
        "mask": laid(mask2),
        "maskT": laid(mask2.T),
        "wqT": by_pairs(L0_xattn_W_q),
        "wkT": by_pairs(L0_xattn_W_k),
        "wvT": laid(np.asarray(L0_xattn_W_v).T),
        "woT": laid(np.asarray(L0_xattn_W_o).T),
        "routerT": laid(np.asarray(L0_ffn_router_w).T),
        "downT": laid(np.asarray(L0_ffn_lora_down).reshape(E * R, D).T),
        "upT": laid(np.asarray(L0_ffn_lora_up).transpose(0, 2, 1).reshape(E * R, D)),
        "ident": np.eye(P, dtype=np.float32),
        "tri": np.tril(np.ones((E, E), np.float32), -1).reshape(1, E * E),
    }
    nc = bacc.Bacc("TRN2", target_bir_lowering=False, num_devices=1)
    args = [nc.dram_tensor(n, a.shape, mybir.dt.from_np(a.dtype), kind="ExternalInput").ap()
            for n, a in arrays.items()]
    out = nc.dram_tensor("out", (NB * S, D), F32, kind="ExternalOutput").ap()
    build(nc, *args, out)
    r = run_bass_kernel_spmd(nc, [arrays], core_ids=[0])
    return r.results[0]["out"].reshape(NB, S, D)
```
